# Optimizing a Trainium2 kernel written in Bass

```python
import numpy as np
import jax
import jax.numpy as jnp

def _softmax(x, axis=-1):
    return jax.nn.softmax(x, axis=axis)

def _gelu(x):
    return jax.nn.gelu(x, approximate=True)

def _silu(x):
    return jax.nn.silu(x)

def _sigmoid(x):
    return jax.nn.sigmoid(x)

def _layernorm(x, axis=-1, eps=1e-05):
    m = jnp.mean(x, axis=axis, keepdims=True)
    v = jnp.var(x, axis=axis, keepdims=True)
    return (x - m) / jnp.sqrt(v + eps)

def _scatter_add(tgt, idx, src, axis=0):
    return tgt.at[idx].add(src)

def _segment_sum(src, seg, n):
    return jax.ops.segment_sum(src, seg, n)
kernel_name = 'mk_adj_preln_d4_adj_r2_67400a'

def setup_inputs(seed: int=0):
    np.random.seed(seed)
    _w = jnp.asarray

    def _rec_inputs():
        import jax
        import jax.numpy as jnp
        _gk = jax.random.key(seed)
        x = -0.0005207 + 1.001 * jax.random.normal(jax.random.fold_in(_gk, 1), (8, 1024, 128), jnp.float32)
        _a = jax.random.bernoulli(jax.random.fold_in(_gk, 2), 0.015625, (1024, 1024))
        adj = _a.astype(jnp.int32)
        return (x, adj)
    x, adj = _rec_inputs()

    def _L0_gnn_setup():
        import jax, jax.numpy as jnp
        import numpy as np
        import math
        CHUNK = 128
        NUM_HEADS = 4
        EPS = 1e-05
        key = jax.random.key(seed)
        ks = jax.random.split(key, 12)
        B, N, F = (4, 1024, 128)
        x = jax.random.normal(ks[0], (B, N, F), dtype=jnp.float32)
        adj_matrix = jax.random.randint(ks[1], (N, N), 0, 2, dtype=jnp.int32)
        s = 1.0 / math.sqrt(F)
        Wq = jax.random.normal(ks[2], (F, F), dtype=jnp.float32) * s
        bq = jnp.zeros((F,), dtype=jnp.float32)
        Wk = jax.random.normal(ks[3], (F, F), dtype=jnp.float32) * s
        bk = jnp.zeros((F,), dtype=jnp.float32)
        Wv = jax.random.normal(ks[4], (F, F), dtype=jnp.float32) * s
        bv = jnp.zeros((F,), dtype=jnp.float32)
        Wo = jax.random.normal(ks[5], (F, F), dtype=jnp.float32) * s
        bo = jnp.zeros((F,), dtype=jnp.float32)
        gamma = jnp.ones((F,), dtype=jnp.float32)
        beta = jnp.zeros((F,), dtype=jnp.float32)
        return {'x': x, 'adj_matrix': adj_matrix, 'Wq': Wq, 'bq': bq, 'Wk': Wk, 'bk': bk, 'Wv': Wv, 'bv': bv, 'Wo': Wo, 'bo': bo, 'gamma': gamma, 'beta': beta}
    _L0_gnn_all = _L0_gnn_setup()
    _L0_gnn_in = {k: v for k, v in _L0_gnn_all.items() if k in ('Wq', 'bq', 'Wk', 'bk', 'Wv', 'bv', 'Wo', 'bo', 'gamma', 'beta')}
    del _L0_gnn_all

    def _L1_gnn_setup():
        import jax, jax.numpy as jnp
        import numpy as np
        ALPHA = 0.2
        key = jax.random.key(seed)
        k1, k2, k3, k4 = jax.random.split(key, 4)
        B, N, Din, Dout = (8, 1024, 128, 128)
        h = jax.random.normal(k1, (B, N, Din), dtype=jnp.float32)
        adj = jax.random.randint(k2, (N, N), 0, 2, dtype=jnp.int32)
        w_bound = float(np.sqrt(6.0 / (Din + Dout)))
        a_bound = float(np.sqrt(6.0 / (2 * Dout + 1)))
        W = jax.random.uniform(k3, (Din, Dout), dtype=jnp.float32, minval=-w_bound, maxval=w_bound)
        a = jax.random.uniform(k4, (2 * Dout, 1), dtype=jnp.float32, minval=-a_bound, maxval=a_bound)
        return {'h': h, 'adj': adj, 'W': W, 'a': a}
    _L1_gnn_all = _L1_gnn_setup()
    _L1_gnn_in = {k: v for k, v in _L1_gnn_all.items() if k in ('W', 'a')}
    del _L1_gnn_all

    def _L2_gnn_setup():
        import jax, jax.numpy as jnp
        import numpy as np
        B, N, D_IN, D_OUT, H = (64, 256, 128, 128, 4)
        HD = D_OUT // H
        key = jax.random.key(seed)
        ks = jax.random.split(key, 10)
        x = jax.random.normal(ks[0], (B, N, D_IN), dtype=jnp.float32)
        adj = jax.random.randint(ks[1], (N, N), 0, 2, dtype=jnp.int32)
        adj = adj.at[jnp.arange(N), jnp.arange(N)].set(1)
        s_in = 1.0 / np.sqrt(D_IN)
        s_out = 1.0 / np.sqrt(D_OUT)
        wq = jax.random.uniform(ks[2], (D_OUT, D_IN), jnp.float32, -s_in, s_in)
        bq = jax.random.uniform(ks[3], (D_OUT,), jnp.float32, -s_in, s_in)
        wk = jax.random.uniform(ks[4], (D_OUT, D_IN), jnp.float32, -s_in, s_in)
        bk = jax.random.uniform(ks[5], (D_OUT,), jnp.float32, -s_in, s_in)
        wv = jax.random.uniform(ks[6], (D_OUT, D_IN), jnp.float32, -s_in, s_in)
        bv = jax.random.uniform(ks[7], (D_OUT,), jnp.float32, -s_in, s_in)
        wo = jax.random.uniform(ks[8], (D_OUT, D_OUT), jnp.float32, -s_out, s_out)
        bo = jax.random.uniform(ks[9], (D_OUT,), jnp.float32, -s_out, s_out)
        return {'x': x, 'adj': adj, 'wq': wq, 'bq': bq, 'wk': wk, 'bk': bk, 'wv': wv, 'bv': bv, 'wo': wo, 'bo': bo}
    _L2_gnn_all = _L2_gnn_setup()
    _L2_gnn_in = {k: v for k, v in _L2_gnn_all.items() if k in ('wq', 'bq', 'wk', 'bk', 'wv', 'bv', 'wo', 'bo')}
    del _L2_gnn_all

    def _L3_gnn_setup():
        import jax, jax.numpy as jnp
        import numpy as np
        ALPHA = 0.2
        EPS = 1e-06
        key = jax.random.key(seed)
        ks = jax.random.split(key, 8)
        B, N, D, H = (2, 1024, 128, 8)
        dh = D // H
        x = jax.random.normal(ks[0], (B, N, D), dtype=jnp.float32)
        adj = jax.random.randint(ks[1], (N, N), 0, 2, dtype=jnp.int32)
        adj = jnp.maximum(adj, jnp.eye(N, dtype=jnp.int32))
        p = jax.random.uniform(ks[2], (B, N, N), dtype=jnp.float32)
        prior = p / jnp.sum(p, axis=-1, keepdims=True)
        W = jax.random.normal(ks[3], (H, D, dh), dtype=jnp.float32) * (1.0 / np.sqrt(D))
        a_src = jax.random.normal(ks[4], (H, dh), dtype=jnp.float32) * (1.0 / np.sqrt(dh))
        a_dst = jax.random.normal(ks[5], (H, dh), dtype=jnp.float32) * (1.0 / np.sqrt(dh))
        beta_tilde = jnp.ones((), dtype=jnp.float32)
        W_out = jax.random.normal(ks[6], (D, D), dtype=jnp.float32) * (1.0 / np.sqrt(D))
        return {'x': x, 'adj': adj, 'prior': prior, 'W': W, 'a_src': a_src, 'a_dst': a_dst, 'beta_tilde': beta_tilde, 'W_out': W_out}
    _L3_gnn_all = _L3_gnn_setup()
    _L3_gnn_in = {k: v for k, v in _L3_gnn_all.items() if k in ('W', 'a_src', 'a_dst', 'beta_tilde', 'W_out')}
    del _L3_gnn_all
    return {'x': x, 'adj': adj, 'L0_gnn_Wq': _L0_gnn_in['Wq'], 'L0_gnn_bq': _L0_gnn_in['bq'], 'L0_gnn_Wk': _L0_gnn_in['Wk'], 'L0_gnn_bk': _L0_gnn_in['bk'], 'L0_gnn_Wv': _L0_gnn_in['Wv'], 'L0_gnn_bv': _L0_gnn_in['bv'], 'L0_gnn_Wo': _L0_gnn_in['Wo'], 'L0_gnn_bo': _L0_gnn_in['bo'], 'L0_gnn_gamma': _L0_gnn_in['gamma'], 'L0_gnn_beta': _L0_gnn_in['beta'], 'L1_gnn_W': _L1_gnn_in['W'], 'L1_gnn_a': _L1_gnn_in['a'], 'L2_gnn_wq': _L2_gnn_in['wq'], 'L2_gnn_bq': _L2_gnn_in['bq'], 'L2_gnn_wk': _L2_gnn_in['wk'], 'L2_gnn_bk': _L2_gnn_in['bk'], 'L2_gnn_wv': _L2_gnn_in['wv'], 'L2_gnn_bv': _L2_gnn_in['bv'], 'L2_gnn_wo': _L2_gnn_in['wo'], 'L2_gnn_bo': _L2_gnn_in['bo'], 'L3_gnn_W': _L3_gnn_in['W'], 'L3_gnn_a_src': _L3_gnn_in['a_src'], 'L3_gnn_a_dst': _L3_gnn_in['a_dst'], 'L3_gnn_beta_tilde': _L3_gnn_in['beta_tilde'], 'L3_gnn_W_out': _L3_gnn_in['W_out']}

def reference(x, adj, L0_gnn_Wq, L0_gnn_bq, L0_gnn_Wk, L0_gnn_bk, L0_gnn_Wv, L0_gnn_bv, L0_gnn_Wo, L0_gnn_bo, L0_gnn_gamma, L0_gnn_beta, L1_gnn_W, L1_gnn_a, L2_gnn_wq, L2_gnn_bq, L2_gnn_wk, L2_gnn_bk, L2_gnn_wv, L2_gnn_bv, L2_gnn_wo, L2_gnn_bo, L3_gnn_W, L3_gnn_a_src, L3_gnn_a_dst, L3_gnn_beta_tilde, L3_gnn_W_out):
    import jax
    import jax.numpy as jnp

    def _L0_gnn_ref(x, adj_matrix, Wq, bq, Wk, bk, Wv, bv, Wo, bo, gamma, beta):
        import jax, jax.numpy as jnp
        import numpy as np
        import math
        CHUNK = 128
        NUM_HEADS = 4
        EPS = 1e-05
        B, N, Fin = x.shape
        H = NUM_HEADS
        Dout = Wq.shape[0]
        Dh = Dout // H
        Nc = N // CHUNK
        q = (x @ Wq.T + bq).reshape(B, N, H, Dh).transpose(0, 2, 1, 3)
        k = (x @ Wk.T + bk).reshape(B, N, H, Dh).transpose(0, 2, 1, 3)
        v = (x @ Wv.T + bv).reshape(B, N, H, Dh).transpose(0, 2, 1, 3)
        kc = k.reshape(B, H, Nc, CHUNK, Dh)
        vc = v.reshape(B, H, Nc, CHUNK, Dh)
        scores = jnp.einsum('bhnd,bhjcd->bhnjc', q, kc) / jnp.sqrt(jnp.asarray(Dh, dtype=q.dtype))
        scores = jnp.clip(scores, -10.0, 10.0)
        mask = adj_matrix.reshape(N, Nc, CHUNK)[None, None]
        scores = jnp.where(mask == 0, jnp.asarray(-10.0, scores.dtype), scores)
        attn = jax.nn.softmax(scores, axis=-1)
        ctx = jnp.einsum('bhnjc,bhjcd->bhnd', attn, vc)
        ctx = ctx.transpose(0, 2, 1, 3).reshape(B, N, Dout)
        out = ctx @ Wo.T + bo
        out = out + x
        mu = jnp.mean(out, axis=-1, keepdims=True)
        var = jnp.mean(jnp.square(out - mu), axis=-1, keepdims=True)
        out = (out - mu) * jax.lax.rsqrt(var + EPS) * gamma + beta
        return out

    def _L1_gnn_ref(h, adj, W, a):
        import jax, jax.numpy as jnp
        import numpy as np
        ALPHA = 0.2
        Wh = jnp.matmul(h, W)
        D = W.shape[1]
        e_src = jnp.matmul(Wh, a[:D])
        e_dst = jnp.matmul(Wh, a[D:])
        e = e_src + jnp.swapaxes(e_dst, 1, 2)
        e = jnp.where(e > 0, e, ALPHA * e)
        mask = (adj > 0)[None, :, :]
        e = jnp.where(mask, e, -jnp.inf)
        alpha_w = jax.nn.softmax(e, axis=-1)
        h_prime = jnp.matmul(alpha_w, Wh)
        return jax.nn.elu(h_prime)

    def _L2_gnn_ref(x, adj, wq, bq, wk, bk, wv, bv, wo, bo):
        import jax, jax.numpy as jnp
        import numpy as np
        B, N, D_IN, D_OUT, H = (64, 256, 128, 128, 4)
        HD = D_OUT // H
        b, n, _ = x.shape
        q = (x @ wq.T + bq).reshape(b, n, H, HD).transpose(0, 2, 1, 3)
        k = (x @ wk.T + bk).reshape(b, n, H, HD).transpose(0, 2, 1, 3)
        v = (x @ wv.T + bv).reshape(b, n, H, HD).transpose(0, 2, 1, 3)
        scores = jnp.einsum('bhnd,bhmd->bhnm', q, k) / jnp.sqrt(jnp.float32(HD))
        scores = jnp.where(adj[None, None] == 0, -jnp.inf, scores)
        attn = jnp.nan_to_num(jax.nn.softmax(scores, axis=-1), nan=0.0)
        out = jnp.einsum('bhnm,bhmd->bhnd', attn, v)
        out = out.transpose(0, 2, 1, 3).reshape(b, n, D_OUT)
        return out @ wo.T + bo

    def _L3_gnn_ref(x, adj, prior, W, a_src, a_dst, beta_tilde, W_out):
        import jax, jax.numpy as jnp
        import numpy as np
        ALPHA = 0.2
        EPS = 1e-06
        B, N, D = x.shape
        x_proj = jnp.einsum('bnd,hdf->bhnf', x, W)
        e_src = jnp.einsum('bhnf,hf->bhn', x_proj, a_src)
        e_dst = jnp.einsum('bhnf,hf->bhn', x_proj, a_dst)
        e = jax.nn.leaky_relu(e_src[..., :, None] + e_dst[..., None, :], ALPHA)
        beta = jax.nn.softplus(beta_tilde)
        e = e + (beta * jnp.log(prior + EPS))[:, None, :, :]
        neg_inf = jnp.finfo(e.dtype).min
        e = jnp.where(adj[None, None, :, :] > 0, e, neg_inf)
        attn = jax.nn.softmax(e, axis=-1)
        h = jnp.einsum('bhij,bhjf->bhif', attn, x_proj)
        h = h.transpose(0, 2, 1, 3).reshape(B, N, D)
        return h @ W_out.T
    h = jnp.maximum(_layernorm(x, axis=-1), 0.0)
    x = x + _L0_gnn_ref(h, adj, L0_gnn_Wq, L0_gnn_bq, L0_gnn_Wk, L0_gnn_bk, L0_gnn_Wv, L0_gnn_bv, L0_gnn_Wo, L0_gnn_bo, L0_gnn_gamma, L0_gnn_beta)
    h = jnp.maximum(_layernorm(x, axis=-1), 0.0)
    x = x + _L1_gnn_ref(h, adj, L1_gnn_W, L1_gnn_a)
    h = jnp.maximum(_layernorm(x, axis=-1), 0.0)
    x = x + _L2_gnn_ref(h, adj, L2_gnn_wq, L2_gnn_bq, L2_gnn_wk, L2_gnn_bk, L2_gnn_wv, L2_gnn_bv, L2_gnn_wo, L2_gnn_bo)
    h = jnp.maximum(_layernorm(x, axis=-1), 0.0)
    x = x + _L3_gnn_ref(h, adj, adj[None], L3_gnn_W, L3_gnn_a_src, L3_gnn_a_dst, L3_gnn_beta_tilde, L3_gnn_W_out)
    return x

_drawn_inputs = setup_inputs


def setup_inputs(seed=0):
    import zlib

    import numpy as np

    out = dict(_drawn_inputs(seed))
    spreads = {'L0_gnn_bq': (0.0, 0.8),
     'L0_gnn_bk': (0.0, 2.0),
     'L0_gnn_bv': (0.0, 0.1),
     'L0_gnn_bo': (0.0, 0.41),
     'L0_gnn_gamma': (1.0, 0.2),
     'L0_gnn_beta': (0.0, 0.1)}
    factors = {'L2_gnn_wq': 8.0,
     'L2_gnn_bq': 21.922,
     'L2_gnn_wk': 8.0,
     'L2_gnn_bk': 64.0,
     'L2_gnn_bv': 3.152,
     'L3_gnn_a_src': 3.456}
    for name, (base, spread) in spreads.items():
        noise = np.random.default_rng([zlib.crc32(name.encode()), seed]).standard_normal(out[name].shape)
        drawn = base * np.exp(spread * noise) if base else spread * noise
        out[name] = jnp.asarray(drawn.astype(out[name].dtype))
    for name, factor in factors.items():
        out[name] = (out[name] * factor).astype(out[name].dtype)
    return out
```

```python
from contextlib import ExitStack

import numpy as np

import concourse.bass as bass
from concourse import mybir

F32 = mybir.dt.float32
BF16 = mybir.dt.bfloat16
I32 = mybir.dt.int32
ACT = mybir.ActivationFunctionType
ALU = mybir.AluOpType
AX = mybir.AxisListType

P = 128
B, N, D = 8, 1024, 128
T = N // P
HALF = 512
NH = N // HALF
H0, DH0 = 4, 32
H3, DH3 = 8, 16
SLOT3 = 32
RING = 6
SCALE = 1.0 / float(np.sqrt(DH0))
E_HI, E_LO = float(np.exp(10.0)), float(np.exp(-10.0))
BIG = 1e38
FLOOR = -1e30
ALPHA = 0.2
PRIOR_EPS = 1e-6
LN_EPS = 1e-5
EXP_AND_LN = 6
UNITS0 = 2 * NH * T
CHUNKS0 = NH * T
UNITS2 = T * H0
UNITS3 = H3 * T
CHUNKS3 = UNITS3 // 4

INPUTS = ["x", "adj", "L0_gnn_Wq", "L0_gnn_bq", "L0_gnn_Wk", "L0_gnn_bk", "L0_gnn_Wv", "L0_gnn_bv",
          "L0_gnn_Wo", "L0_gnn_bo", "L0_gnn_gamma", "L0_gnn_beta", "L1_gnn_W", "L1_gnn_a",
          "L2_gnn_wq", "L2_gnn_bq", "L2_gnn_wk", "L2_gnn_bk", "L2_gnn_wv", "L2_gnn_bv", "L2_gnn_wo",
          "L2_gnn_bo", "L3_gnn_W", "L3_gnn_a_src", "L3_gnn_a_dst", "L3_gnn_beta_tilde", "L3_gnn_W_out"]

SQUARE = ["L0_gnn_Wq", "L0_gnn_Wk", "L0_gnn_Wv", "L0_gnn_Wo", "L2_gnn_wq", "L2_gnn_wk", "L2_gnn_wv",
          "L2_gnn_wo", "L3_gnn_W_out"]
WQ, WK, WV, WO = 0, 1, 2, 3
WOUT3 = 8
COLS = ["L0_gnn_bq", "L0_gnn_bk", "L2_gnn_bq", "L2_gnn_bk"]
ROWS = ["L0_gnn_bv", "L0_gnn_bo", "L0_gnn_gamma", "L0_gnn_beta", "L2_gnn_bv", "L2_gnn_bo"]
BV0, BO0, GAMMA, BETA, BV2, BO2 = range(6)



class Links:

    def __init__(self, eng, sem):
        self.eng, self.sem, self.n = eng, sem, 0

    def __call__(self, ins):
        self.n += 1
        ins.then_inc(self.sem, 1)
        self.eng.wait_ge(self.sem, self.n)


def blocks(ap):
    return ap.rearrange("p (t d) -> p t d", d=P)


def spread(ap, n):
    return ap.unsqueeze(2).broadcast_to((ap.shape[0], ap.shape[1], n))


def repeat(ap, n):
    return ap.unsqueeze(1).broadcast_to((ap.shape[0], n, ap.shape[1]))


def build(nc, a, scratch, out):
    with ExitStack() as ctx:
        def sb(name, shape, dt=F32):
            return ctx.enter_context(nc.sbuf_tensor(name, shape, dt))

        def sem(name):
            return ctx.enter_context(nc.semaphore(name))

        clipU = sb("clipU", [P, T, N])
        prior = sb("prior", [P, T, N])
        mask1 = sb("mask1", [P, T, N], BF16)
        maskN = sb("maskN", [P, T, N], BF16)
        wT = sb("wT", [P, len(SQUARE), P])
        w1 = sb("w1", [P, P + 1])
        w1s = sb("w1s", [P, P])
        w1d = sb("w1d", [P, P])
        w3 = sb("w3", [P, P + H3])
        w3s = sb("w3s", [P, H3])
        cols = sb("cols", [P, len(COLS)])
        rows = sb("rows", [P, len(ROWS), P])
        wa1 = sb("wa1", [P, 2])
        ident = sb("ident", [P, P])
        ones = sb("ones", [P, P])
        c32 = sb("c32", [P, 1])
        beta3 = sb("beta3", [P, 4])
        rowmax = sb("rowmax", [P, T])
        empty3 = sb("empty3", [P, T])
        amax = sb("amax", [P, 8])
        xin = sb("xin", [P, N])
        xs = sb("xs", [P, N])
        hn = sb("hn", [P, N])
        hT = sb("hT", [P, N])
        qz = sb("qz", [P, H0, N])
        kT = sb("kT", [P, N])
        vn = sb("vn", [P, N])
        ring = sb("ring", [P, RING + H0, N])
        pT = ring[:, RING:RING + H0, :]
        RING3 = RING + 2
        tA, tB, tC = (sb(n, [P, N]) for n in ("tA", "tB", "tC"))
        a1b = tC[:, 0:2 * P]
        a3b = tC[:, 2 * P:4 * P].rearrange("p (k c) -> p k c", k=2)
        ring3 = [ring[:, i, :] for i in range(RING)] + [hT[:], tC[:]]
        v3 = sb("v3", [P, T, H3, SLOT3])
        bnst = sb("bnst", [P, T, 6])
        mv = sb("mv", [P, T, 2])
        veps, lnv, isd, nwt, rstd = (sb(n, [P, T]) for n in ("veps", "lnv", "isd", "nwt", "rstd"))
        dmax1 = sb("dmax1", [P, 1])
        dm1, b1, d1, nb1, rz1 = (kT[:, i * T:(i + 1) * T] for i in range(5))
        nm2, z2, rz2 = (tC[:, i * UNITS2:(i + 1) * UNITS2] for i in range(3))
        dmax3 = sb("dmax3", [H3, 1])
        diag3 = sb("diag3", [H3, H3])
        dmaxb3 = sb("dmaxb3", [P, H3])
        sv3 = vn[:, 0:H3 * SLOT3]
        dm3, b3, d3, nb3, rz3 = (kT[:, i * T * H3:(i + 1) * T * H3] for i in range(5))
        dm3, b3, d3, nb3 = (t.rearrange("p (t h) -> p t h", h=H3) for t in (dm3, b3, d3, nb3))
        rz3 = rz3.rearrange("p (g w) -> p g w", g=2)

        psum = ctx.enter_context(nc.psum_tensor("psum", [P, 3, N], F32))
        acc = ctx.enter_context(nc.psum_tensor("acc", [P, NH, HALF], F32))
        slot = [psum[:, i, :] for i in range(3)]
        lnz = tA[:, 0:HALF]
        rzs = tB[:].rearrange("p (r c) -> p r c", r=2)
        part0 = tC[:].rearrange("p (r c) -> p r c", r=2)
        ctx0 = xs

        S = {n: sem(n) for n in """weights_in adj_in x_in x_stored go_pe go_act go_v go_pool consts wt_psum wt_copied wa_ready
             amax_t amax_tr amax_row amax_b adjf adjT_psum adjT_read g_lin g_log beta_e beta_ready
             dve_setup_link act_setup_link pool_link""".split()}
        per_graph = {n: sem(n) for n in """var_ready isd_ready h_ready hT_psum hT_ready xin_used
             q_psum k_psum v_psum qz_zero qz_ready kT_ready v_ready
             s0_ready e0_done p0_ready pv0_done z0_read rz0_ready ctx0_read ctx0_added o0_psum
             d1_psum s1_psum v1_psum dmax1_ready s1_shifted v1_ready dm1_ready r1_ready b1_ready nb1_ready
             t1_ready p1_ready pv1_done z1_done u1_ready n1_psum neg1_ready e1_ready
             s2_ready nm2_ready p2_ready t2_psum t2_even t2_odd pv2_done c2_ready cn2_psum cn2_ready
             cT2_psum cT2_ready o2_psum
             d3_psum s3_psum v3_psum dmax3_ready s3_shifted r3_ready r3_stored r3_in0 r3_in1 r3_in2 r3_in3 r3_in4 r3_in5 r3_in6 r3_in7 v3_ready
             dmaxb3_psum dm3_ready b3_ready nb3_ready sum3_psum t3_ready p3_ready pv3_done o3_ready
             on3_psum cn3_ready cT3_psum cT3_ready o3_psum x_done turn_over biased dve_link act_link""".split()}
        S.update(per_graph)
        numbers = sorted(s.num for s in per_graph.values())
        assert numbers == list(range(numbers[0], numbers[-1] + 1))
        block = ctx.enter_context(nc.Block())

        def end_graph(eng, go):
            eng.sem_inc(S["turn_over"], 1)
            eng.wait_ge(S[go], 1)
            eng.sem_clear(S[go])

        @block.sync
        def _(sp):
            with nc.allow_non_contiguous_dma("weights, once"):
                sp.dma_start(prior[:].bitcast(I32), a["adj"].rearrange("(t p) n -> p t n", p=P)).then_inc(S["adj_in"], 16)
                sp.dma_start(xin[:].rearrange("p (t d) -> p t d", d=D),
                             a["x"][0, :, :].rearrange("(t p) d -> p t d", p=P)).then_inc(S["x_in"], 16)
                for i, n in enumerate(SQUARE):
                    sp.dma_start(qz[:, 0, :][:, i * P:(i + 1) * P] if i < 8 else qz[:, 1, 0:P],
                                 a[n]).then_inc(S["weights_in"], 16)
                sp.dma_start(w1[:, 0:P], a["L1_gnn_W"]).then_inc(S["weights_in"], 16)
                sp.dma_start(w3[:, 0:P].rearrange("p (h f) -> p h f", h=H3),
                             a["L3_gnn_W"].rearrange("h d f -> d h f")).then_inc(S["weights_in"], 16)
                sp.dma_start(a1b, a["L1_gnn_a"].rearrange("(o n) c -> o (n c)", o=1).broadcast_to((P, 2 * P))).then_inc(S["weights_in"], 16)
                for i, n in enumerate(["L3_gnn_a_src", "L3_gnn_a_dst"]):
                    sp.dma_start(a3b[:, i, :], a[n].rearrange("(o h) f -> o (h f)", o=1).broadcast_to((P, P))).then_inc(S["weights_in"], 16)
                for i, n in enumerate(COLS):
                    sp.dma_start(cols[:, i:i + 1], a[n].rearrange("(p o) -> p o", o=1)).then_inc(S["weights_in"], 16)
                for i, n in enumerate(ROWS):
                    sp.dma_start(rows[:, i, :], a[n].rearrange("(o n) -> o n", o=1).broadcast_to((P, P))).then_inc(S["weights_in"], 16)
                sp.dma_start(beta3[:, 0:1], a["L3_gnn_beta_tilde"].broadcast_to((P, 1))).then_inc(S["weights_in"], 16)
            sp.sem_inc(S["x_stored"], 16)
            with sp.Fori(0, B) as b:
                sp.wait_ge(S["xin_used"], 1)
                nxt = (b + 1) % B
                sp.dma_start(xin[:].rearrange("p (t d) -> p t d", d=D),
                             a["x"][bass.ds(nxt, 1), :, :].rearrange("o (t p) d -> p (o t) d", p=P)).then_inc(S["x_in"], 16)
                sp.wait_ge(S["r3_ready"], 1)
                sp.dma_start(scratch[:, :], tB[0:H3, :]).then_inc(S["r3_stored"], 16)
                sp.wait_ge(S["r3_stored"], 16)
                for h in range(H3):
                    sp.dma_start(pT[:, h, :] if h < 4 else qz[:, h - 4, :],
                                 scratch[h:h + 1, :].broadcast_to((P, N))).then_inc(S[f"r3_in{h}"], 16)
                sp.wait_ge(S["x_done"], 1)
                sp.dma_start(out[bass.ds(b, 1), :, :].rearrange("o (t p) d -> p (o t) d", p=P),
                             xs[:].rearrange("p (t d) -> p t d", d=D)).then_inc(S["x_stored"], 16)
                sp.wait_ge(S["turn_over"], 4)
                sp.sem_clear(range(numbers[0], numbers[-1] + 1))
                for name in ("go_pe", "go_act", "go_v", "go_pool"):
                    sp.sem_inc(S[name], 1)
            sp.wait_ge(S["x_stored"], 16)
            sp.wait_ge(S["x_in"], 16)

        n_weights = 16 * (len(SQUARE) + 2 + 1 + 2 + len(COLS) + len(ROWS) + 1)

        @block.gpsimd
        def _(pool):
            pool.memset(ident[:], 0.0).then_inc(S["pool_link"], 1)
            pool.wait_ge(S["pool_link"], 1)
            pool.affine_select(out=ident[:], in_=ident[:], compare_op=ALU.not_equal, fill=1.0, base=0,
                               pattern=[[-1, P]], channel_multiplier=1).then_inc(S["pool_link"], 1)
            pool.wait_ge(S["pool_link"], 2)
            pool.memset(ones[:], 1.0)
            pool.memset(c32[:], 1.0 / 32)
            pool.memset(v3[:], 0.0).then_inc(S["pool_link"], 1)
            pool.wait_ge(S["pool_link"], 3)
            pool.memset(v3[:, :, :, DH3:DH3 + 1], 1.0).then_inc(S["consts"], 1)
            adds = CHUNKS0 - NH
            pool.wait_ge(S["wt_copied"], 1)
            with pool.Fori(0, B) as b:
                pool.memset(qz[:], 0.0).then_inc(S["qz_zero"], 1)
                pool.wait_ge(S["hT_psum"], 1)
                pool.tensor_tensor(blocks(hn[:]), blocks(hn[:]), repeat(rows[:, BO0, :], T), ALU.add)
                pool.tensor_tensor(blocks(xin[:]), blocks(xin[:]), repeat(rows[:, BETA, :], T),
                                   ALU.add).then_inc(S["biased"], 1)
                for m in range(CHUNKS0):
                    if m % T:
                        half = slice(m // T * HALF, (m // T + 1) * HALF)
                        pool.wait_ge(S["ctx0_read"], m + 1)
                        if m % T > 1:
                            pool.wait_ge(S["ctx0_added"], m - m // T - 1)
                        pool.tensor_tensor(ctx0[:, half], ctx0[:, half], part0[:, m % 2, :],
                                           ALU.add).then_inc(S["ctx0_added"], 1)
                pool.wait_ge(S["h_ready"], 3)
                pool.tensor_tensor(blocks(xs[:]), blocks(xs[:]), repeat(rows[:, BO2, :], T),
                                   ALU.add).then_inc(S["biased"], 1)
                end_graph(pool, "go_pool")

        @block.tensor
        def _(pe):
            mm = nc.tensor.matmul

            def transpose_blocks(dst, src):
                for t in range(T):
                    last = nc.tensor.transpose(dst[:, t * P:(t + 1) * P], src[:, t * P:(t + 1) * P], ident[:])
                return last

            pe.wait_ge(S["consts"], 1)
            pe.wait_ge(S["weights_in"], n_weights)
            last = transpose_blocks(slot[0], qz[:, 0, :])
            nc.tensor.transpose(slot[1][:, 0:P], qz[:, 1, 0:P], ident[:]).then_inc(S["wt_psum"], 1)
            pe.wait_ge(S["amax_t"], 1)
            nc.tensor.transpose(acc[0:1, 0, 0:P], amax[:, 0:1], ident[:]).then_inc(S["amax_tr"], 1)
            pe.wait_ge(S["amax_row"], 1)
            mm(acc[:, 1, 0:1], ones[0:1, :], amax[0:1, 1:2], start=True, stop=True).then_inc(S["amax_b"], 1)
            pe.wait_ge(S["wt_copied"], 1)
            for c in range(T):
                if c >= 3:
                    pe.wait_ge(S["adjT_read"], c - 2)
                for t in range(T):
                    last = nc.tensor.transpose(slot[c % 3][:, t * P:(t + 1) * P],
                                               ring[:, t, c * P:(c + 1) * P], ident[:])
                last.then_inc(S["adjT_psum"], 1)
            pe.wait_ge(S["adjT_read"], T)
            pe.wait_ge(S["wa_ready"], 1)

            def h_transposed(b, layer):
                pe.wait_ge(S["h_ready"], layer + 1)
                transpose_blocks(slot[0], hn).then_inc(S["hT_psum"], 1)
                pe.wait_ge(S["hT_ready"], layer + 1)

            def project_T(dst, w):
                for i in range(NH):
                    last = mm(dst[:, i * HALF:(i + 1) * HALF], w, hT[:, i * HALF:(i + 1) * HALF],
                              start=True, stop=True)
                return last

            def project_rows(dst, lhs, w):
                for t in range(T):
                    last = mm(dst[:, t * P:(t + 1) * P], lhs[:, t * P:(t + 1) * P], w, start=True, stop=True)
                return last

            def qkv(b, k):
                project_T(slot[1], wT[:, 4 * k + WQ, :]).then_inc(S["q_psum"], 1)
                project_T(slot[2], wT[:, 4 * k + WK, :]).then_inc(S["k_psum"], 1)
                project_rows(slot[0], hT, wT[:, 4 * k + WV, :]).then_inc(S["v_psum"], 1)
                pe.wait_ge(S["qz_ready"], k + 1)
                pe.wait_ge(S["kT_ready"], k + 1)
                pe.wait_ge(S["v_ready"], k + 1)

            def layer0(b):
                def scores(u):
                    n, pair = u // 2, u % 2
                    half, c = n // T, n % T
                    if u >= 3:
                        pe.wait_ge(S["e0_done"], u - 2)
                    for i in range(2):
                        last = mm(slot[u % 3][:, i * HALF:(i + 1) * HALF], kT[:, c * P:(c + 1) * P],
                                  qz[:, 2 * pair + i, half * HALF:(half + 1) * HALF], start=True, stop=True)
                    last.then_inc(S["s0_ready"], 1)

                def values(m):
                    c = m % T
                    pe.wait_ge(S["p0_ready"], 2 * m + 2)
                    if m >= 1:
                        pe.wait_ge(S["ctx0_read"], m)
                        pe.wait_ge(S["z0_read"], m)
                    for k in range(2):
                        for h in range(H0):
                            lhs = vn[:, c * P + h * DH0:c * P + (h + 1) * DH0] if k == 0 else ones[:, 0:DH0]
                            last = mm(acc[h * DH0:(h + 1) * DH0, k, :], lhs,
                                      ring[:, (2 * m + h // 2) % RING, (h % 2) * HALF:(h % 2 + 1) * HALF],
                                      start=True, stop=True)
                    last.then_inc(S["pv0_done"], 1)

                for n in range(CHUNKS0):
                    scores(2 * n)
                    scores(2 * n + 1)
                    if n:
                        values(n - 1)
                values(CHUNKS0 - 1)
                pe.wait_ge(S["ctx0_read"], CHUNKS0)
                pe.wait_ge(S["ctx0_added"], CHUNKS0 - NH)
                project_rows(slot[0], ctx0, wT[:, WO, :]).then_inc(S["o0_psum"], 1)

            def layer1(b):
                project_T(slot[1], w1d[:]).then_inc(S["d1_psum"], 1)
                project_T(slot[2], w1s[:]).then_inc(S["s1_psum"], 1)
                for t in range(T):
                    if t == T // 2:
                        pe.wait_ge(S["dmax1_ready"], 1)
                    last = mm(psum[:, t // 4, t % 4 * 256:t % 4 * 256 + P + 1], hT[:, t * P:(t + 1) * P], w1[:],
                              start=True, stop=True)
                last.then_inc(S["v1_psum"], 1)
                pe.wait_ge(S["v1_ready"], 1)
                for c in range(T):
                    pe.wait_ge(S["p1_ready"], c + 1)
                    for i in range(NH):
                        last = mm(acc[:, i, :], vn[:, c * P:(c + 1) * P], ring[:, c % RING, i * HALF:(i + 1) * HALF],
                                  start=(c == 0), stop=(c == T - 1))
                    last.then_inc(S["pv1_done"], 1)
                    if c % 4 == 3:
                        for i in range(NH):
                            for q in range(4):
                                last = mm(psum[32 * q:32 * q + 32, 2, i * HALF:(i + 1) * HALF], ones[:, 0:32],
                                          ring[:, (c - 3 + q) % RING, i * HALF:(i + 1) * HALF],
                                          start=(c == 3), stop=(c == T - 1))
                        last.then_inc(S["z1_done"], 1)
                pe.wait_ge(S["u1_ready"], 1)
                transpose_blocks(slot[0], tA)
                for t in range(T):
                    last = mm(slot[1][:, t:t + 1], tC[:, t * P:(t + 1) * P], c32[:], start=True, stop=True)
                last.then_inc(S["n1_psum"], 1)

            def s_slot(w):
                return 0 if w == 0 else (2 * w - 1) % 3

            def t_slot(w):
                return (2 * w + 2) % 3

            def layer2(b):
                def scores(w):
                    blk, h = w // H0, w % H0
                    if w == 2:
                        pe.wait_ge(S["p2_ready"], 1)
                    if w >= 3:
                        pe.wait_ge(S["t2_even"], w - 2)
                        pe.wait_ge(S["t2_odd"], w - 2)
                    for i in range(NH):
                        cs = slice(i * HALF, (i + 1) * HALF)
                        last = mm(slot[s_slot(w)][:, cs], qz[:, h, blk * P:(blk + 1) * P], kT[:, cs],
                                  start=True, stop=True)
                    last.then_inc(S["s2_ready"], 1)

                def transposed(w):
                    pe.wait_ge(S["p2_ready"], w + 1)
                    transpose_blocks(slot[t_slot(w)], ring[:, w % RING, :]).then_inc(S["t2_psum"], 1)

                def values(blk):
                    pe.wait_ge(S["t2_even"], H0 * (blk + 1))
                    pe.wait_ge(S["t2_odd"], H0 * (blk + 1))
                    for c in range(T):
                        for h in range(H0):
                            last = mm(acc[h * DH0:(h + 1) * DH0, blk // 4, blk % 4 * P:(blk % 4 + 1) * P],
                                      vn[:, c * P + h * DH0:c * P + (h + 1) * DH0], pT[:, h, c * P:(c + 1) * P],
                                      start=(c == 0), stop=(c == T - 1))
                    last.then_inc(S["pv2_done"], 1)

                scores(0)
                for w in range(UNITS2):
                    if w + 1 < UNITS2:
                        scores(w + 1)
                    if w and w % H0 == 0:
                        values(w // H0 - 1)
                    transposed(w)
                values(T - 1)
                pe.wait_ge(S["c2_ready"], 1)
                transpose_blocks(slot[0], tA).then_inc(S["cn2_psum"], 1)
                pe.wait_ge(S["cn2_ready"], 1)
                transpose_blocks(slot[1], tB).then_inc(S["cT2_psum"], 1)
                pe.wait_ge(S["cT2_ready"], 1)
                project_rows(slot[2], tC, wT[:, 4 + WO, :]).then_inc(S["o2_psum"], 1)

            def layer3(b):
                for s, w, name in ((1, w3[:, P:P + H3], "d3_psum"), (2, w3s[:], "s3_psum")):
                    for i in range(NH):
                        cs = slice(i * HALF, (i + 1) * HALF)
                        last = mm(psum[0:H3, s, cs], w, hT[:, cs], start=True, stop=True)
                    last.then_inc(S[name], 1)
                for t in range(T):
                    if t == T // 2:
                        pe.wait_ge(S["dmax3_ready"], 1)
                    last = mm(psum[:, t // 4, t % 4 * 256:t % 4 * 256 + P + H3], hT[:, t * P:(t + 1) * P], w3[:],
                              start=True, stop=True)
                last.then_inc(S["v3_psum"], 1)
                mm(acc[:, 0, 0:H3], ones[0:H3, :], diag3[:], start=True, stop=True).then_inc(S["dmaxb3_psum"], 1)
                pe.wait_ge(S["s3_shifted"], 1)
                pe.wait_ge(S["v3_ready"], 1)
                for c in range(T):
                    last = mm(psum[:, 2, 0:H3 * SLOT3], ones[:], v3[:, c, :, :].rearrange("p h f -> p (h f)"),
                              start=(c == 0), stop=(c == T - 1))
                last.then_inc(S["sum3_psum"], 1)
                for n in range(CHUNKS3):
                    g, c = n // T, n % T
                    pe.wait_ge(S["p3_ready"], 4 * n + 4)
                    if n == T:
                        pe.wait_ge(S["o3_ready"], 1)
                    for i in range(NH):
                        for h in range(4):
                            last = mm(acc[32 * h:32 * h + 32, i, :], v3[:, c, 4 * g + h, :],
                                      ring3[(4 * n + h) % RING3][:, i * HALF:(i + 1) * HALF],
                                      start=(c == 0), stop=(c == T - 1))
                    last.then_inc(S["pv3_done"], 1)
                    if n == T:
                        transpose_blocks(slot[0], tA).then_inc(S["on3_psum"], 1)
                pe.wait_ge(S["o3_ready"], 2)
                transpose_blocks(slot[1], tC).then_inc(S["on3_psum"], 1)
                pe.wait_ge(S["cn3_ready"], 1)
                transpose_blocks(slot[2], hn).then_inc(S["cT3_psum"], 1)
                pe.wait_ge(S["cT3_ready"], 1)
                project_rows(slot[0], tA, wT[:, WOUT3, :]).then_inc(S["o3_psum"], 1)

            with pe.Fori(0, B) as b:
                h_transposed(b, 0)
                qkv(b, 0)
                layer0(b)
                h_transposed(b, 1)
                layer1(b)
                h_transposed(b, 2)
                qkv(b, 1)
                layer2(b)
                h_transposed(b, 3)
                layer3(b)
                end_graph(pe, "go_pe")

        @block.scalar
        def _(act):
            link = Links(act, S["act_setup_link"])
            go = nc.scalar.activation
            act.add_instruction(mybir.InstLoadActFuncSet(act_func_set_id=EXP_AND_LN, name=nc.get_next_instruction_name(),
                                                         engine=mybir.EngineType.Activation))

            act.wait_ge(S["wt_psum"], 1)
            go(wT[:, 0:8, :].rearrange("p w o -> p (w o)"), slot[0], ACT.Copy)
            go(wT[:, 8, :], slot[1][:, 0:P], ACT.Copy).then_inc(S["wt_copied"], 1)
            act.wait_ge(S["weights_in"], n_weights)
            act.wait_ge(S["beta_e"], 1)
            link(go(beta3[:, 1:2], beta3[:, 1:2], ACT.Exp, scale=-1.0))
            go(beta3[:, 1:2], beta3[:, 1:2], ACT.Ln, bias=1.0).then_inc(S["beta_ready"], 1)
            act.wait_ge(S["beta_e"], 2)
            act.wait_ge(S["adjf"], 2)
            for c in range(T):
                act.wait_ge(S["g_lin"], c + 1)
                link(go(prior[:, c, :], prior[:, c, :], ACT.Ln, scale=amax[:, 3:4], bias=amax[:, 4:5]))
                go(prior[:, c, :], prior[:, c, :], ACT.Exp, scale=beta3[:, 2:3]).then_inc(S["g_log"], 1)

            def inverse_deviation(b, n):
                act.wait_ge(S["var_ready"], n + 1)
                link(go(lnv[:], veps[:], ACT.Ln))
                go(isd[:], lnv[:], ACT.Exp, scale=-0.5).then_inc(S["isd_ready"], 1)

            def h_transposed(b, layer):
                act.wait_ge(S["hT_psum"], layer + 1)
                go(hT[:], slot[0], ACT.Copy).then_inc(S["hT_ready"], 1)

            def spread_q(b, k):
                act.wait_ge(S["q_psum"], k + 1)
                act.wait_ge(S["qz_zero"], 1)
                for h in range(H0):
                    ps = slice(h * DH0, (h + 1) * DH0)
                    last = go(qz[ps, h, :], psum[ps, 1, :], ACT.Identity, bias=cols[ps, 2 * k:2 * k + 1])
                last.then_inc(S["qz_ready"], 1)

            def layer0(b):
                def weights(u):
                    act.wait_ge(S["s0_ready"], u + 1)
                    if u >= RING:
                        act.wait_ge(S["pv0_done"], (u - RING) // 2 + 1)
                    go(ring[:, u % RING, :], slot[u % 3], ACT.Exp, scale=SCALE).then_inc(S["e0_done"], 1)

                def inverse_sums(m):
                    act.wait_ge(S["pv0_done"], m + 1)
                    link(go(lnz, acc[:, 1, :], ACT.Ln))
                    act.sem_inc(S["z0_read"], 1)
                    if m >= 2:
                        act.wait_ge(S["ctx0_read"], m - 1)
                    go(rzs[:, m % 2, :], lnz, ACT.Exp, scale=-1.0).then_inc(S["rz0_ready"], 1)

                for n in range(CHUNKS0):
                    if n >= 2:
                        inverse_sums(n - 2)
                    weights(2 * n)
                    weights(2 * n + 1)
                inverse_sums(CHUNKS0 - 2)
                inverse_sums(CHUNKS0 - 1)

            def layer1(b):
                act.wait_ge(S["s1_shifted"], 1)
                go(tB[:], tA[:], ACT.Exp, scale=-(1 - ALPHA)).then_inc(S["r1_ready"], 1)
                act.wait_ge(S["dm1_ready"], 1)
                go(b1, dm1, ACT.Exp)
                go(d1, dm1, ACT.Exp, scale=ALPHA).then_inc(S["b1_ready"], 1)
                act.wait_ge(S["nb1_ready"], 1)
                act.wait_ge(S["r1_ready"], 1)
                act.wait_ge(S["b1_ready"], 1)
                for c in range(T):
                    if c >= RING:
                        act.wait_ge(S["pv1_done"], c - RING + 1)
                        act.wait_ge(S["z1_done"], 1)
                    go(ring[:, c % RING, :], tB[:], ACT.Relu, scale=d1[:, c:c + 1],
                       bias=nb1[:, c:c + 1]).then_inc(S["t1_ready"], 1)
                act.wait_ge(S["pv1_done"], T)
                act.wait_ge(S["z1_done"], 2)
                go(tA[:], acc[:].rearrange("p i c -> p (i c)"), ACT.Copy)
                go(tC[:], slot[2], ACT.Copy).then_inc(S["u1_ready"], 1)
                act.wait_ge(S["neg1_ready"], 1)
                go(tC[:], tC[:], ACT.Exp).then_inc(S["e1_ready"], 1)

            def layer2(b):
                def weights(w):
                    act.wait_ge(S["nm2_ready"], w + 1)
                    if w >= RING:
                        act.wait_ge(S["t2_psum"], w - RING + 1)
                    go(ring[:, w % RING, :], slot[0 if w == 0 else (2 * w - 1) % 3], ACT.Exp, scale=-1.0,
                       bias=nm2[:, w:w + 1], accum_out=z2[:, w:w + 1]).then_inc(S["p2_ready"], 1)

                def copy_odd(w):
                    act.wait_ge(S["t2_psum"], w + 1)
                    if w >= H0:
                        act.wait_ge(S["pv2_done"], w // H0)
                    go(pT[:, w % H0, HALF:N], psum[:, (2 * w + 2) % 3, HALF:N], ACT.Copy).then_inc(S["t2_odd"], 1)

                for w in range(UNITS2):
                    weights(w)
                    if w:
                        copy_odd(w - 1)
                copy_odd(UNITS2 - 1)
                act.wait_ge(S["pv2_done"], T)
                go(tA[:], acc[:].rearrange("p i c -> p (i c)"), ACT.Copy).then_inc(S["c2_ready"], 1)
                act.wait_ge(S["cT2_psum"], 1)
                go(tC[:], slot[1], ACT.Copy).then_inc(S["cT2_ready"], 1)

            def layer3(b):
                act.wait_ge(S["s3_shifted"], 1)
                go(tB[0:H3, :], tA[0:H3, :], ACT.Exp, scale=-(1 - ALPHA)).then_inc(S["r3_ready"], 1)
                act.wait_ge(S["dm3_ready"], 1)
                go(b3, dm3, ACT.Exp)
                go(d3, dm3, ACT.Exp, scale=ALPHA).then_inc(S["b3_ready"], 1)
                act.wait_ge(S["nb3_ready"], 1)
                act.wait_ge(S["b3_ready"], 1)
                for v in range(UNITS3):
                    g, c, h = v // (4 * T), v // 4 % T, v // (4 * T) * 4 + v % 4
                    if c == 0:
                        act.wait_ge(S[f"r3_in{h}"], 16)
                    if v == 4 * T + 4:
                        act.wait_ge(S["pv3_done"], T)
                        go(tA[:], acc[:].rearrange("p i c -> p (i c)"), ACT.Copy).then_inc(S["o3_ready"], 1)
                    if v >= RING3:
                        act.wait_ge(S["pv3_done"], (v - RING3) // 4 + 1)
                    fac = pT[:, h, :] if g == 0 else qz[:, h - 4, :]
                    go(ring3[v % RING3], fac, ACT.Relu, scale=d3[:, c, h:h + 1],
                       bias=nb3[:, c, h:h + 1]).then_inc(S["t3_ready"], 1)
                act.wait_ge(S["pv3_done"], CHUNKS3)
                go(tC[:], acc[:].rearrange("p i c -> p (i c)"), ACT.Copy).then_inc(S["o3_ready"], 1)
                act.wait_ge(S["cT3_psum"], 1)
                go(tA[:], slot[2], ACT.Copy).then_inc(S["cT3_ready"], 1)

            link = Links(act, S["act_link"])
            with act.Fori(0, B) as b:
                inverse_deviation(b, 0)
                h_transposed(b, 0)
                spread_q(b, 0)
                layer0(b)
                inverse_deviation(b, 1)
                inverse_deviation(b, 2)
                h_transposed(b, 1)
                layer1(b)
                inverse_deviation(b, 3)
                h_transposed(b, 2)
                spread_q(b, 1)
                layer2(b)
                inverse_deviation(b, 4)
                h_transposed(b, 3)
                layer3(b)
                end_graph(act, "go_act")

        @block.vector
        def _(v):
            link = Links(v, S["dve_setup_link"])

            af = ring[:, 0:T, :]
            v.wait_ge(S["adj_in"], 16)
            link(v.tensor_copy(af, prior[:].bitcast(I32)))
            link(v.tensor_reduce(rowmax[:], af, AX.X, ALU.max))
            v.tensor_reduce(amax[:, 0:1], rowmax[:], AX.X, ALU.max).then_inc(S["amax_t"], 1)
            v.tensor_scalar(maskN[:], af, 0.0, -BIG, ALU.is_equal, ALU.mult)
            v.tensor_scalar(empty3[:], rowmax[:], 0.0, None, ALU.is_le)
            v.wait_ge(S["weights_in"], n_weights)
            link(v.tensor_tensor(tA[:, 0:P], w1[:, 0:P], a1b[:, 0:P], ALU.mult))
            v.tensor_tensor(tA[:, P:2 * P], w1[:, 0:P], a1b[:, P:2 * P], ALU.mult)
            v.tensor_tensor(tB[:, 0:P], w3[:, 0:P], a3b[:, 0, :], ALU.mult)
            link(v.tensor_tensor(tB[:, P:2 * P], w3[:, 0:P], a3b[:, 1, :], ALU.mult))
            v.tensor_reduce(wa1[:], tA[:, 0:2 * P].rearrange("p (k o) -> p k o", k=2), AX.X, ALU.add)
            v.tensor_reduce(w3s[:], tB[:, 0:P].rearrange("p (h f) -> p h f", h=H3), AX.X, ALU.add)
            link(v.tensor_reduce(w3[:, P:P + H3], tB[:, P:2 * P].rearrange("p (h f) -> p h f", h=H3), AX.X, ALU.add))
            v.wait_ge(S["consts"], 1)
            v.tensor_copy(w1[:, P:P + 1], wa1[:, 1:2])
            v.tensor_scalar(w1s[:], ones[:], wa1[:, 0:1], None, ALU.mult)
            v.tensor_scalar(w1d[:], ones[:], wa1[:, 1:2], None, ALU.mult).then_inc(S["wa_ready"], 1)
            link(v.tensor_scalar(beta3[:, 1:2], beta3[:, 0:1], -1.0, None, ALU.mult))
            v.tensor_scalar(beta3[:, 3:4], beta3[:, 0:1], 0.0, None, ALU.max)
            link(v.tensor_tensor(beta3[:, 1:2], beta3[:, 1:2], beta3[:, 0:1], ALU.max))
            v.sem_inc(S["beta_e"], 1)
            v.wait_ge(S["beta_ready"], 1)
            v.tensor_tensor(beta3[:, 2:3], beta3[:, 1:2], beta3[:, 3:4], ALU.add).then_inc(S["beta_e"], 1)
            v.wait_ge(S["amax_tr"], 1)
            v.tensor_reduce(amax[0:1, 1:2], acc[0:1, 0, 0:P], AX.X, ALU.max).then_inc(S["amax_row"], 1)
            v.wait_ge(S["amax_b"], 1)
            link(v.tensor_scalar(amax[:, 2:3], acc[:, 1, 0:1], 0.0, PRIOR_EPS, ALU.max, ALU.add))
            link(v.reciprocal(amax[:, 3:4], amax[:, 2:3]))
            link(v.tensor_scalar(amax[:, 4:5], amax[:, 3:4], PRIOR_EPS, None, ALU.mult))
            v.sem_inc(S["adjf"], 2)
            for c in range(T):
                v.wait_ge(S["adjT_psum"], c + 1)
                v.tensor_scalar(prior[:, c, :], slot[c % 3], 0.0, None, ALU.max).then_inc(S["g_lin"], 1)
                v.tensor_scalar(mask1[:, c, :], slot[c % 3], 0.0, None, ALU.is_gt)
                link(v.tensor_scalar(clipU[:, c, :], slot[c % 3], 0.0, E_HI, ALU.not_equal, ALU.mult))
                v.sem_inc(S["adjT_read"], 1)
                v.tensor_scalar(clipU[:, c, :], clipU[:, c, :], E_LO, None, ALU.max)
            for c in range(T):
                v.wait_ge(S["g_log"], c + 1)
                last = v.tensor_tensor(prior[:, c, :], prior[:, c, :], mask1[:, c, :], ALU.mult)
            link(last)

            def norm_stats(b, n, src):
                for t in range(T):
                    last = v.bn_stats(bnst[:, t, :], src[:, t * P:(t + 1) * P])
                link(last)
                for t in range(T):
                    last = v.bn_aggr(mv[:, t, :], bnst[:, t, :])
                link(last)
                v.tensor_scalar(veps[:], mv[:, :, 1], LN_EPS, None, ALU.add).then_inc(S["var_ready"], 1)
                v.wait_ge(S["isd_ready"], n + 1)
                link(v.tensor_tensor(nwt[:], isd[:], isd[:], ALU.mult))
                link(v.scalar_tensor_tensor(out=nwt[:], in0=nwt[:], scalar=-0.5, in1=veps[:], op0=ALU.mult, op1=ALU.mult))
                link(v.scalar_tensor_tensor(out=rstd[:], in0=nwt[:], scalar=1.5, in1=isd[:], op0=ALU.add, op1=ALU.mult))

            def norm_apply(dst, src):
                for t in range(T):
                    cs = slice(t * P, (t + 1) * P)
                    last = v.tensor_scalar(dst[:, cs], src[:, cs], mv[:, t, 0:1], rstd[:, t:t + 1],
                                           ALU.subtract, ALU.mult)
                link(last)

            def pre_norm(b, n, src):
                norm_stats(b, n, src)
                norm_apply(hn, src)
                v.tensor_scalar(hn[:], hn[:], 0.0, None, ALU.max).then_inc(S["h_ready"], 1)

            def keys_values(b, k):
                v.wait_ge(S["k_psum"], k + 1)
                v.tensor_scalar(kT[:], slot[2], cols[:, 2 * k + 1:2 * k + 2], None, ALU.add).then_inc(S["kT_ready"], 1)
                v.wait_ge(S["v_psum"], k + 1)
                v.tensor_tensor(blocks(vn[:]), blocks(slot[0]), repeat(rows[:, (BV0, BV2)[k], :], T),
                                ALU.add).then_inc(S["v_ready"], 1)

            def layer0(b):
                adds = CHUNKS0 - NH
                v.wait_ge(S["x_stored"], 16)
                v.sem_clear(S["x_stored"])

                def clip(u):
                    n = u // 2
                    half, c = n // T, n % T
                    v.wait_ge(S["e0_done"], u + 1)
                    tile = ring[:, u % RING, :].rearrange("p (i c) -> p i c", i=2)
                    v.scalar_tensor_tensor(out=tile, in0=tile, scalar=E_LO,
                                           in1=repeat(clipU[:, c, half * HALF:(half + 1) * HALF], 2),
                                           op0=ALU.max, op1=ALU.min).then_inc(S["p0_ready"], 1)

                def scale(m):
                    v.wait_ge(S["rz0_ready"], m + 1)
                    half = slice(m // T * HALF, (m // T + 1) * HALF)
                    if m % T and m >= 2 and (m - 2) % T:
                        v.wait_ge(S["ctx0_added"], (m - 2) - (m - 2) // T)
                    dst = part0[:, m % 2, :] if m % T else ctx0[:, half]
                    v.tensor_tensor(dst, acc[:, 0, :], rzs[:, m % 2, :], ALU.mult).then_inc(S["ctx0_read"], 1)

                for n in range(CHUNKS0):
                    if n >= 2:
                        scale(n - 2)
                    clip(2 * n)
                    clip(2 * n + 1)
                scale(CHUNKS0 - 2)
                scale(CHUNKS0 - 1)
                v.wait_ge(S["biased"], 1)
                v.wait_ge(S["o0_psum"], 1)
                link(v.tensor_tensor(tA[:], slot[0], hn[:], ALU.add))
                norm_stats(b, 1, tA)
                norm_apply(tA, tA)
                link(v.tensor_tensor(blocks(tA[:]), blocks(tA[:]), repeat(rows[:, GAMMA, :], T), ALU.mult))
                link(v.tensor_tensor(xs[:], xin[:], tA[:], ALU.add))
                v.sem_inc(S["xin_used"], 1)

            def layer1(b):
                v.wait_ge(S["d1_psum"], 1)
                link(v.tensor_reduce(dmax1[:], slot[1], AX.X, ALU.max))
                v.sem_inc(S["dmax1_ready"], 1)
                v.wait_ge(S["s1_psum"], 1)
                v.tensor_scalar(tA[:], slot[2], dmax1[:, 0:1], -100.0, ALU.add, ALU.max).then_inc(S["s1_shifted"], 1)
                v.wait_ge(S["v1_psum"], 1)
                view = psum[:, 0:2, :].rearrange("p s (k c) -> p (s k) c", c=256)
                v.tensor_scalar(dm1, view[:, :, P], dmax1[:, 0:1], None, ALU.subtract).then_inc(S["dm1_ready"], 1)
                v.tensor_copy(blocks(vn[:]), view[:, :, 0:P]).then_inc(S["v1_ready"], 1)
                v.wait_ge(S["b1_ready"], 1)
                v.tensor_scalar(nb1, b1, -1.0, None, ALU.mult).then_inc(S["nb1_ready"], 1)
                for c in range(T):
                    v.wait_ge(S["t1_ready"], c + 1)
                    v.scalar_tensor_tensor(out=ring[:, c % RING, :], in0=ring[:, c % RING, :], scalar=b1[:, c:c + 1],
                                           in1=mask1[:, c, :], op0=ALU.add, op1=ALU.mult).then_inc(S["p1_ready"], 1)
                v.wait_ge(S["n1_psum"], 1)
                link(v.reciprocal(rz1, slot[1][:, 0:T]))
                link(v.tensor_tensor(blocks(tA[:]), blocks(slot[0]), spread(rz1, P), ALU.mult))
                v.tensor_scalar(tC[:], tA[:], 0.0, None, ALU.min).then_inc(S["neg1_ready"], 1)
                link(v.tensor_scalar(tA[:], tA[:], 0.0, None, ALU.max))
                v.wait_ge(S["e1_ready"], 1)
                link(v.scalar_tensor_tensor(out=tA[:], in0=tC[:], scalar=-1.0, in1=tA[:], op0=ALU.add, op1=ALU.add))
                link(v.tensor_tensor(xs[:], xs[:], tA[:], ALU.add))

            def layer2(b):
                def row_max(w):
                    v.wait_ge(S["s2_ready"], w + 1)
                    tile = slot[0 if w == 0 else (2 * w - 1) % 3]
                    v.tensor_tensor_reduce(out=tile, in0=tile, in1=maskN[:, w // H0, :], scale=-SCALE, scalar=-FLOOR,
                                           op0=ALU.add, op1=ALU.min,
                                           accum_out=nm2[:, w:w + 1]).then_inc(S["nm2_ready"], 1)

                def copy_even(w):
                    v.wait_ge(S["t2_psum"], w + 1)
                    if w >= H0:
                        v.wait_ge(S["pv2_done"], w // H0)
                    v.tensor_copy(pT[:, w % H0, 0:HALF], psum[:, (2 * w + 2) % 3, 0:HALF]).then_inc(S["t2_even"], 1)

                for w in range(UNITS2):
                    row_max(w)
                    if w:
                        copy_even(w - 1)
                copy_even(UNITS2 - 1)
                v.wait_ge(S["p2_ready"], UNITS2)
                link(v.tensor_scalar(z2, z2, 1e-30, None, ALU.max))
                link(v.reciprocal(rz2, z2))
                v.wait_ge(S["cn2_psum"], 1)
                v.tensor_tensor(tB[:].rearrange("p (w d) -> p w d", d=DH0),
                                slot[0].rearrange("p (w d) -> p w d", d=DH0), spread(rz2, DH0),
                                ALU.mult).then_inc(S["cn2_ready"], 1)
                v.wait_ge(S["o2_psum"], 1)
                v.wait_ge(S["biased"], 2)
                link(v.tensor_tensor(xs[:], xs[:], slot[2], ALU.add))

            def layer3(b):
                v.wait_ge(S["d3_psum"], 1)
                link(v.tensor_reduce(dmax3[:], psum[0:H3, 1, :], AX.X, ALU.max))
                v.tensor_scalar(diag3[:], ident[0:H3, 0:H3], dmax3[:, 0:1], None, ALU.mult).then_inc(S["dmax3_ready"], 1)
                v.wait_ge(S["s3_psum"], 1)
                v.tensor_scalar(tA[0:H3, :], psum[0:H3, 2, :], dmax3[:, 0:1], -100.0, ALU.add,
                                ALU.max).then_inc(S["s3_shifted"], 1)
                v.wait_ge(S["v3_psum"], 1)
                view = psum[:, 0:2, :].rearrange("p s (k c) -> p (s k) c", c=256)
                v.tensor_copy(v3[:, :, :, 0:DH3], view[:, :, 0:P].rearrange("p t (h f) -> p t h f", h=H3)).then_inc(S["v3_ready"], 1)
                v.wait_ge(S["dmaxb3_psum"], 1)
                link(v.tensor_copy(dmaxb3[:], acc[:, 0, 0:H3]))
                v.tensor_tensor(dm3, view[:, :, P:P + H3], repeat(dmaxb3[:], T), ALU.subtract).then_inc(S["dm3_ready"], 1)
                v.wait_ge(S["b3_ready"], 1)
                v.tensor_scalar(nb3, b3, -1.0, None, ALU.mult).then_inc(S["nb3_ready"], 1)
                v.wait_ge(S["sum3_psum"], 1)
                link(v.tensor_copy(sv3, psum[:, 2, 0:H3 * SLOT3]))

                def normalise(g):
                    v.wait_ge(S["on3_psum"], g + 1)
                    for t in range(T):
                        last = v.scalar_tensor_tensor(out=tB[:, t * P:(t + 1) * P], in0=sv3[:, g * P:(g + 1) * P],
                                                      scalar=empty3[:, t:t + 1], in1=slot[g][:, t * P:(t + 1) * P],
                                                      op0=ALU.mult, op1=ALU.add)
                    link(last)
                    nat = tB[:].rearrange("p (w c) -> p w c", c=SLOT3)
                    link(v.reciprocal(rz3[:, g, :], nat[:, :, DH3]))
                    for t in range(T):
                        last = v.tensor_tensor(
                            hn[:, t * P + g * 64:t * P + g * 64 + 64].rearrange("p (h f) -> p h f", h=4),
                            nat[:, 4 * t:4 * t + 4, 0:DH3], spread(rz3[:, g, 4 * t:4 * t + 4], DH3), ALU.mult)
                    return last

                for u in range(UNITS3):
                    g, c, h = u // (4 * T), u // 4 % T, u // (4 * T) * 4 + u % 4
                    v.wait_ge(S["t3_ready"], u + 1)
                    v.scalar_tensor_tensor(out=ring3[u % RING3], in0=ring3[u % RING3], scalar=b3[:, c, h:h + 1],
                                           in1=prior[:, c, :], op0=ALU.add, op1=ALU.mult).then_inc(S["p3_ready"], 1)
                    if u == 4 * T + 12:
                        link(normalise(0))
                normalise(1).then_inc(S["cn3_ready"], 1)
                v.wait_ge(S["o3_psum"], 1)
                link(v.tensor_tensor(xs[:], xs[:], slot[0], ALU.add))
                v.sem_inc(S["x_done"], 1)

            link = Links(v, S["dve_link"])
            with v.Fori(0, B) as b:
                v.wait_ge(S["x_in"], 16)
                v.sem_clear(S["x_in"])
                pre_norm(b, 0, xin)
                keys_values(b, 0)
                layer0(b)
                pre_norm(b, 2, xs)
                layer1(b)
                pre_norm(b, 3, xs)
                keys_values(b, 1)
                layer2(b)
                pre_norm(b, 4, xs)
                layer3(b)
                end_graph(v, "go_v")


def kernel(**inputs):
    import concourse.bacc as bacc
    from concourse.bass_utils import run_bass_kernel_spmd

    nc = bacc.Bacc("TRN2", target_bir_lowering=False, num_devices=1)
    arrays, aps = {}, {}
    for name in INPUTS:
        arr = np.ascontiguousarray(inputs[name])
        if arr.ndim == 0:
            arr = arr.reshape(1, 1)
        arrays[f"in_{name}"] = arr
        aps[name] = nc.dram_tensor(f"in_{name}", arr.shape, mybir.dt.from_np(arr.dtype), kind="ExternalInput").ap()
    scratch = nc.dram_tensor("row_factors", (H3, N), F32).ap()
    out = nc.dram_tensor("out_0", (B, N, D), F32, kind="ExternalOutput").ap()
    build(nc, aps, scratch, out)
    r = run_bass_kernel_spmd(nc, [arrays], core_ids=[0])
    return r.results[0]["out_0"]
```

```python
from contextlib import ExitStack

import numpy as np

import concourse.bass as bass
from concourse import mybir

F32 = mybir.dt.float32
BF16 = mybir.dt.bfloat16
I32 = mybir.dt.int32
ACT = mybir.ActivationFunctionType
ALU = mybir.AluOpType
AX = mybir.AxisListType

P = 128
B, N, D = 8, 1024, 128
T = N // P
HALF = 512
NH = N // HALF
H0, DH0 = 4, 32
H3, DH3 = 8, 16
SLOT3 = 32
RING = 6
SCALE = 1.0 / float(np.sqrt(DH0))
E_HI, E_LO = float(np.exp(10.0)), float(np.exp(-10.0))
BIG = 1e38
FLOOR = -1e30
ALPHA = 0.2
PRIOR_EPS = 1e-6
LN_EPS = 1e-5
EXP_AND_LN = 6
UNITS0 = 2 * NH * T
CHUNKS0 = NH * T
O0_AT = 24
NEXT_NORM_AT = 8
UNITS2 = T * H0
UNITS3 = H3 * T
CHUNKS3 = UNITS3 // 4

INPUTS = ["x", "adj", "L0_gnn_Wq", "L0_gnn_bq", "L0_gnn_Wk", "L0_gnn_bk", "L0_gnn_Wv", "L0_gnn_bv",
          "L0_gnn_Wo", "L0_gnn_bo", "L0_gnn_gamma", "L0_gnn_beta", "L1_gnn_W", "L1_gnn_a",
          "L2_gnn_wq", "L2_gnn_bq", "L2_gnn_wk", "L2_gnn_bk", "L2_gnn_wv", "L2_gnn_bv", "L2_gnn_wo",
          "L2_gnn_bo", "L3_gnn_W", "L3_gnn_a_src", "L3_gnn_a_dst", "L3_gnn_beta_tilde", "L3_gnn_W_out"]

SQUARE = ["L0_gnn_Wq", "L0_gnn_Wk", "L0_gnn_Wv", "L0_gnn_Wo", "L2_gnn_wq", "L2_gnn_wk", "L2_gnn_wv",
          "L2_gnn_wo", "L3_gnn_W_out"]
WQ, WK, WV, WO = 0, 1, 2, 3
WOUT3 = 8
COLS = ["L0_gnn_bq", "L0_gnn_bk", "L2_gnn_bq", "L2_gnn_bk"]
ROWS = ["L0_gnn_bv", "L0_gnn_bo", "L0_gnn_gamma", "L0_gnn_beta", "L2_gnn_bv", "L2_gnn_bo"]
BV0, BO0, GAMMA, BETA, BV2, BO2 = range(6)



class Links:

    def __init__(self, eng, sem):
        self.eng, self.sem, self.n = eng, sem, 0

    def __call__(self, ins):
        self.n += 1
        ins.then_inc(self.sem, 1)
        self.eng.wait_ge(self.sem, self.n)


def blocks(ap):
    return ap.rearrange("p (t d) -> p t d", d=P)


def spread(ap, n):
    return ap.unsqueeze(2).broadcast_to((ap.shape[0], ap.shape[1], n))


def repeat(ap, n):
    return ap.unsqueeze(1).broadcast_to((ap.shape[0], n, ap.shape[1]))


def build(nc, a, scratch, out):
    with ExitStack() as ctx:
        def sb(name, shape, dt=F32):
            return ctx.enter_context(nc.sbuf_tensor(name, shape, dt))

        def sem(name):
            return ctx.enter_context(nc.semaphore(name))

        clipU = sb("clipU", [P, T, N])
        prior = sb("prior", [P, T, N])
        mask1 = sb("mask1", [P, T, N], BF16)
        maskN = sb("maskN", [P, T, N], BF16)
        wT = sb("wT", [P, len(SQUARE), P])
        w1 = sb("w1", [P, P + 1])
        w1s = sb("w1s", [P, P])
        w1d = sb("w1d", [P, P])
        w3 = sb("w3", [P, P + H3])
        w3s = sb("w3s", [P, H3])
        cols = sb("cols", [P, len(COLS)])
        rows = sb("rows", [P, len(ROWS), P])
        wa1 = sb("wa1", [P, 2])
        ident = sb("ident", [P, P])
        ones = sb("ones", [P, P])
        c32 = sb("c32", [P, 1])
        beta3 = sb("beta3", [P, 4])
        rowmax = sb("rowmax", [P, T])
        empty3 = sb("empty3", [P, T])
        amax = sb("amax", [P, 8])
        xin = sb("xin", [P, N])
        xs = sb("xs", [P, N])
        hn = sb("hn", [P, N])
        hT = sb("hT", [P, N])
        qz = sb("qz", [P, H0, N])
        kT = sb("kT", [P, N])
        vn = sb("vn", [P, N])
        ring = sb("ring", [P, RING + H0, N])
        pT = ring[:, RING:RING + H0, :]
        RING3 = RING + 2
        tA, tB, tC = (sb(n, [P, N]) for n in ("tA", "tB", "tC"))
        a1b = tC[:, 0:2 * P]
        a3b = tC[:, 2 * P:4 * P].rearrange("p (k c) -> p k c", k=2)
        cn3 = pT[:, 0, :]
        ring3 = [ring[:, i, :] for i in range(RING)] + [hT[:], tC[:]]
        v3 = sb("v3", [P, T, H3, SLOT3])
        bnst = sb("bnst", [P, T, 6])
        mv = sb("mv", [P, T, 2])
        veps, lnv, isd, nwt, rstd = (sb(n, [P, T]) for n in ("veps", "lnv", "isd", "nwt", "rstd"))
        dmax1 = sb("dmax1", [P, 1])
        dm1, b1, d1, nb1, rz1 = (kT[:, i * T:(i + 1) * T] for i in range(5))
        nm2, z2, rz2 = (tC[:, i * UNITS2:(i + 1) * UNITS2] for i in range(3))
        dmax3 = sb("dmax3", [H3, 1])
        diag3 = sb("diag3", [H3, H3])
        dmaxb3 = sb("dmaxb3", [P, H3])
        sv3 = vn[:, 0:H3 * SLOT3]
        dm3, b3, d3, nb3, rz3 = (kT[:, i * T * H3:(i + 1) * T * H3] for i in range(5))
        dm3, b3, d3, nb3 = (t.rearrange("p (t h) -> p t h", h=H3) for t in (dm3, b3, d3, nb3))
        rz3 = rz3.rearrange("p (g w) -> p g w", g=2)

        psum = ctx.enter_context(nc.psum_tensor("psum", [P, 3, N], F32))
        acc = ctx.enter_context(nc.psum_tensor("acc", [P, NH, HALF], F32))
        def slot0(u):
            return (u if u < O0_AT else u + 1) % 3

        slot = [psum[:, i, :] for i in range(3)]
        hx = pT[:, 3, :]
        rzs = tB[:].rearrange("p (r c) -> p r c", r=2)
        part0 = tC[:].rearrange("p (r c) -> p r c", r=2)
        ctx0 = xs

        S = {n: sem(n) for n in """weights_in adj_in x_in x_stored go_pe go_act go_v go_pool consts wt_psum wt_copied wa_ready
             amax_t amax_tr amax_row amax_b adjf adjT_psum adjT_read g_lin g_log beta_e beta_ready
             dve_setup_link act_setup_link var_first isd_first h_first pool_link""".split()}
        per_graph = {n: sem(n) for n in """var_ready isd_ready h_ready hT_psum hT_ready xin_used
             q_psum k_psum v_psum qz_zero qz_ready qz3_ready kT_ready v_ready
             s0_ready e0_done p0_ready pv0_done z0_read rz0_ready ctx0_read ctx0_added o0_psum o0_read
             d1_psum s1_psum v1_psum dmax1_ready s1_shifted v1_ready dm1_ready r1_ready b1_ready nb1_ready
             t1_ready p1_ready pv1_done z1_done u1_ready zc1_ready n1_psum neg1_ready e1_ready
             s2_ready nm2_ready p2_ready t2_psum t2_even t2_odd pv2_done c2_ready cn2_psum cn2_ready
             cT2_psum cT2_ready o2_psum
             d3_psum s3_psum v3_psum dmax3_ready s3_shifted r3_ready r3_stored r3_in0 r3_in1 r3_in2 r3_in3 r3_in4 r3_in5 r3_in6 r3_in7 v3_ready
             dmaxb3_psum dm3_ready b3_ready nb3_ready sum3_psum t3_ready p3_ready pv3_done o3_ready
             on3_psum cn3_ready cT3_psum cT3_ready o3_psum x_done turn_over biased pool_graph_link dve_link act_link""".split()}
        S.update(per_graph)
        numbers = sorted(s.num for s in per_graph.values())
        assert numbers == list(range(numbers[0], numbers[-1] + 1))
        block = ctx.enter_context(nc.Block())

        def end_graph(eng, go):
            eng.sem_inc(S["turn_over"], 1)
            eng.wait_ge(S[go], 1)
            eng.sem_clear(S[go])

        @block.sync
        def _(sp):
            with nc.allow_non_contiguous_dma("weights, once"):
                sp.dma_start(prior[:].bitcast(I32), a["adj"].rearrange("(t p) n -> p t n", p=P)).then_inc(S["adj_in"], 16)
                sp.dma_start(xin[:].rearrange("p (t d) -> p t d", d=D),
                             a["x"][0, :, :].rearrange("(t p) d -> p t d", p=P)).then_inc(S["x_in"], 16)
                for i, n in enumerate(SQUARE):
                    sp.dma_start(qz[:, 0, :][:, i * P:(i + 1) * P] if i < 8 else qz[:, 1, 0:P],
                                 a[n]).then_inc(S["weights_in"], 16)
                sp.dma_start(w1[:, 0:P], a["L1_gnn_W"]).then_inc(S["weights_in"], 16)
                sp.dma_start(w3[:, 0:P].rearrange("p (h f) -> p h f", h=H3),
                             a["L3_gnn_W"].rearrange("h d f -> d h f")).then_inc(S["weights_in"], 16)
                sp.dma_start(a1b, a["L1_gnn_a"].rearrange("(o n) c -> o (n c)", o=1).broadcast_to((P, 2 * P))).then_inc(S["weights_in"], 16)
                for i, n in enumerate(["L3_gnn_a_src", "L3_gnn_a_dst"]):
                    sp.dma_start(a3b[:, i, :], a[n].rearrange("(o h) f -> o (h f)", o=1).broadcast_to((P, P))).then_inc(S["weights_in"], 16)
                for i, n in enumerate(COLS):
                    sp.dma_start(cols[:, i:i + 1], a[n].rearrange("(p o) -> p o", o=1)).then_inc(S["weights_in"], 16)
                for i, n in enumerate(ROWS):
                    sp.dma_start(rows[:, i, :], a[n].rearrange("(o n) -> o n", o=1).broadcast_to((P, P))).then_inc(S["weights_in"], 16)
                sp.dma_start(beta3[:, 0:1], a["L3_gnn_beta_tilde"].broadcast_to((P, 1))).then_inc(S["weights_in"], 16)
            sp.sem_inc(S["x_stored"], 16)
            with sp.Fori(0, B) as b:
                sp.wait_ge(S["xin_used"], 1)
                nxt = (b + 1) % B
                sp.dma_start(xin[:].rearrange("p (t d) -> p t d", d=D),
                             a["x"][bass.ds(nxt, 1), :, :].rearrange("o (t p) d -> p (o t) d", p=P)).then_inc(S["x_in"], 16)
                sp.wait_ge(S["r3_ready"], 1)
                sp.dma_start(scratch[:, :], tB[0:H3, :]).then_inc(S["r3_stored"], 16)
                sp.wait_ge(S["r3_stored"], 16)
                for h in range(H3):
                    sp.dma_start(pT[:, h, :] if h < 4 else qz[:, h - 4, :],
                                 scratch[h:h + 1, :].broadcast_to((P, N))).then_inc(S[f"r3_in{h}"], 16)
                sp.wait_ge(S["x_done"], 1)
                sp.dma_start(out[bass.ds(b, 1), :, :].rearrange("o (t p) d -> p (o t) d", p=P),
                             xs[:].rearrange("p (t d) -> p t d", d=D)).then_inc(S["x_stored"], 16)
                sp.wait_ge(S["turn_over"], 4)
                sp.sem_clear(range(numbers[0], numbers[-1] + 1))
                for name in ("go_pe", "go_act", "go_v", "go_pool"):
                    sp.sem_inc(S[name], 1)
            sp.wait_ge(S["x_stored"], 16)

        n_weights = 16 * (len(SQUARE) + 2 + 1 + 2 + len(COLS) + len(ROWS) + 1)

        @block.gpsimd
        def _(pool):
            pool.memset(ident[:], 0.0).then_inc(S["pool_link"], 1)
            pool.wait_ge(S["pool_link"], 1)
            pool.affine_select(out=ident[:], in_=ident[:], compare_op=ALU.not_equal, fill=1.0, base=0,
                               pattern=[[-1, P]], channel_multiplier=1).then_inc(S["pool_link"], 1)
            pool.wait_ge(S["pool_link"], 2)
            pool.memset(ones[:], 1.0)
            pool.memset(c32[:], 1.0 / 32)
            pool.memset(v3[:], 0.0).then_inc(S["pool_link"], 1)
            pool.wait_ge(S["pool_link"], 3)
            pool.memset(v3[:, :, :, DH3:DH3 + 1], 1.0).then_inc(S["consts"], 1)
            adds = CHUNKS0 - NH
            pool.wait_ge(S["wt_copied"], 1)
            with pool.Fori(0, B) as b:
                pool.memset(qz[:], 0.0).then_inc(S["qz_zero"], 1)
                pool.wait_ge(S["hT_psum"], 2)
                pool.tensor_scalar(hn[:], hn[:], 0.0, None, ALU.max).then_inc(S["pool_graph_link"], 1)
                pool.wait_ge(S["pool_graph_link"], 1)
                pool.tensor_tensor(blocks(hn[:]), blocks(hn[:]), repeat(rows[:, BO0, :], T), ALU.add)
                pool.tensor_tensor(blocks(xin[:]), blocks(xin[:]), repeat(rows[:, BETA, :], T),
                                   ALU.add).then_inc(S["biased"], 1)
                for m in range(CHUNKS0):
                    if m % T:
                        half = slice(m // T * HALF, (m // T + 1) * HALF)
                        pool.wait_ge(S["ctx0_read"], m + 1)
                        if m % T > 1:
                            pool.wait_ge(S["ctx0_added"], m - m // T - 1)
                        pool.tensor_tensor(ctx0[:, half], ctx0[:, half], part0[:, m % 2, :],
                                           ALU.add).then_inc(S["ctx0_added"], 1)
                pool.wait_ge(S["h_ready"], 4)
                pool.tensor_tensor(blocks(xs[:]), blocks(xs[:]), repeat(rows[:, BO2, :], T),
                                   ALU.add).then_inc(S["biased"], 1)
                end_graph(pool, "go_pool")

        @block.tensor
        def _(pe):
            mm = nc.tensor.matmul

            def transpose_blocks(dst, src):
                for t in range(T):
                    last = nc.tensor.transpose(dst[:, t * P:(t + 1) * P], src[:, t * P:(t + 1) * P], ident[:])
                return last

            pe.wait_ge(S["consts"], 1)
            pe.wait_ge(S["weights_in"], n_weights)
            last = transpose_blocks(slot[0], qz[:, 0, :])
            nc.tensor.transpose(slot[1][:, 0:P], qz[:, 1, 0:P], ident[:]).then_inc(S["wt_psum"], 1)
            pe.wait_ge(S["amax_t"], 1)
            nc.tensor.transpose(acc[0:1, 0, 0:P], amax[:, 0:1], ident[:]).then_inc(S["amax_tr"], 1)
            pe.wait_ge(S["amax_row"], 1)
            mm(acc[:, 1, 0:1], ones[0:1, :], amax[0:1, 1:2], start=True, stop=True).then_inc(S["amax_b"], 1)
            pe.wait_ge(S["wt_copied"], 1)
            for c in range(T):
                if c >= 3:
                    pe.wait_ge(S["adjT_read"], c - 2)
                for t in range(T):
                    last = nc.tensor.transpose(slot[c % 3][:, t * P:(t + 1) * P],
                                               ring[:, t, c * P:(c + 1) * P], ident[:])
                last.then_inc(S["adjT_psum"], 1)
            pe.wait_ge(S["adjT_read"], T)
            pe.wait_ge(S["wa_ready"], 1)

            def transpose_half(dst, src, i):
                for t in range(i * T // 2, (i + 1) * T // 2):
                    last = nc.tensor.transpose(dst[:, t * P:(t + 1) * P], src[:, t * P:(t + 1) * P], ident[:])
                return last

            def h_transposed(layer, src):
                for i in range(2):
                    if layer:
                        pe.wait_ge(S["h_ready"], 2 * (layer - 1) + i + 1)
                    transpose_half(slot[0], src, i).then_inc(S["hT_psum"], 1)

            def project_T(layer, dst, w, i):
                pe.wait_ge(S["hT_ready"], 2 * layer + i + 1)
                return mm(dst[:, i * HALF:(i + 1) * HALF], w, hT[:, i * HALF:(i + 1) * HALF],
                          start=True, stop=True)

            def project_rows(dst, lhs, w, i):
                for t in range(i * T // 2, (i + 1) * T // 2):
                    last = mm(dst[:, t * P:(t + 1) * P], lhs[:, t * P:(t + 1) * P], w, start=True, stop=True)
                return last

            def queries_keys(layer, k):
                for i in range(2):
                    q = project_T(layer, slot[1], wT[:, 4 * k + WQ, :], i)
                    last = project_T(layer, slot[2], wT[:, 4 * k + WK, :], i)
                q.then_inc(S["q_psum"], 1)
                last.then_inc(S["k_psum"], 1)
                pe.wait_ge(S["kT_ready"], k + 1)

            def all_queries(k):
                pe.wait_ge(S["qz_ready"], 3 * k + 3)
                pe.wait_ge(S["qz3_ready"], k + 1)

            def project_values(k):
                for i in range(2):
                    last = project_rows(acc[:].rearrange("p i c -> p (i c)"), hT, wT[:, 4 * k + WV, :], i)
                last.then_inc(S["v_psum"], 1)

            def layer0(b):
                def scores(u):
                    n, pair = u // 2, u % 2
                    half, c = n // T, n % T
                    if u == 0:
                        pe.wait_ge(S["qz_ready"], 2)
                    if u == 1:
                        all_queries(0)
                    if u == O0_AT + 2:
                        pe.wait_ge(S["o0_read"], 1)
                    elif u >= 3:
                        pe.wait_ge(S["e0_done"], u - 2 if u < O0_AT or u >= O0_AT + 3 else u - 1)
                    for i in range(2):
                        last = mm(slot[slot0(u)][:, i * HALF:(i + 1) * HALF], kT[:, c * P:(c + 1) * P],
                                  qz[:, 2 * pair + i, half * HALF:(half + 1) * HALF], start=True, stop=True)
                    last.then_inc(S["s0_ready"], 1)

                def values(m):
                    c = m % T
                    pe.wait_ge(S["p0_ready"], 2 * m + 2)
                    if m == 0:
                        pe.wait_ge(S["v_ready"], 1)
                    if m >= 1:
                        pe.wait_ge(S["ctx0_read"], m)
                        pe.wait_ge(S["z0_read"], m)
                    for k in range(2):
                        for h in range(H0):
                            lhs = vn[:, c * P + h * DH0:c * P + (h + 1) * DH0] if k == 0 else ones[:, 0:DH0]
                            last = mm(acc[h * DH0:(h + 1) * DH0, k, :], lhs,
                                      ring[:, (2 * m + h // 2) % RING, (h % 2) * HALF:(h % 2 + 1) * HALF],
                                      start=True, stop=True)
                    last.then_inc(S["pv0_done"], 1)

                for n in range(CHUNKS0):
                    scores(2 * n)
                    scores(2 * n + 1)
                    if n == 0:
                        project_values(0)
                    if 2 * n + 2 == O0_AT:
                        pe.wait_ge(S["ctx0_added"], T - 1)
                        pe.wait_ge(S["ctx0_read"], T)
                        pe.wait_ge(S["e0_done"], O0_AT - 2)
                        project_rows(slot[O0_AT % 3], ctx0, wT[:, WO, :], 0).then_inc(S["o0_psum"], 1)
                    if n:
                        values(n - 1)
                values(CHUNKS0 - 1)
                pe.wait_ge(S["ctx0_read"], CHUNKS0)
                pe.wait_ge(S["ctx0_added"], CHUNKS0 - NH)
                project_rows(slot[0], ctx0, wT[:, WO, :], 1).then_inc(S["o0_psum"], 1)

            def layer1(b):
                for i in range(2):
                    last = project_T(1, slot[1], w1d[:], i)
                last.then_inc(S["d1_psum"], 1)
                for i in range(2):
                    last = project_T(1, slot[2], w1s[:], i)
                last.then_inc(S["s1_psum"], 1)
                for t in range(T):
                    if t == T // 2:
                        pe.wait_ge(S["dmax1_ready"], 1)
                    last = mm(psum[:, t // 4, t % 4 * 256:t % 4 * 256 + P + 1], hT[:, t * P:(t + 1) * P], w1[:],
                              start=True, stop=True)
                last.then_inc(S["v1_psum"], 1)
                pe.wait_ge(S["v1_ready"], 1)
                for c in range(T):
                    pe.wait_ge(S["p1_ready"], c + 1)
                    if c % 4 == 3:
                        for i in range(NH):
                            for q in range(4):
                                last = mm(psum[32 * q:32 * q + 32, 2, i * HALF:(i + 1) * HALF], ones[:, 0:32],
                                          ring[:, (c - 3 + q) % RING, i * HALF:(i + 1) * HALF],
                                          start=(c == 3), stop=(c == T - 1))
                        last.then_inc(S["z1_done"], 1)
                    for i in range(NH):
                        last = mm(acc[:, i, :], vn[:, c * P:(c + 1) * P], ring[:, c % RING, i * HALF:(i + 1) * HALF],
                                  start=(c == 0), stop=(c == T - 1))
                        if c == T - 1 and i == 0:
                            last.then_inc(S["pv1_done"], 1)
                    last.then_inc(S["pv1_done"], 1)
                pe.wait_ge(S["zc1_ready"], 1)
                for t in range(T):
                    mm(slot[1][:, t:t + 1], tC[:, t * P:(t + 1) * P], c32[:], start=True, stop=True)
                for i in range(2):
                    pe.wait_ge(S["u1_ready"], i + 1)
                    transpose_half(slot[0], tA, i).then_inc(S["n1_psum"], 1)

            def s_slot(w):
                return 0 if w == 0 else (2 * w - 1) % 3

            def t_slot(w):
                return (2 * w + 2) % 3

            def layer2(b):
                def scores(w):
                    blk, h = w // H0, w % H0
                    if w == 0:
                        pe.wait_ge(S["qz_ready"], 3 + 1)
                    if w == 1:
                        all_queries(1)
                    if w == 2:
                        pe.wait_ge(S["p2_ready"], 1)
                    if w >= 3:
                        pe.wait_ge(S["t2_even"], w - 2)
                        pe.wait_ge(S["t2_odd"], w - 2)
                    for i in range(NH):
                        cs = slice(i * HALF, (i + 1) * HALF)
                        last = mm(slot[s_slot(w)][:, cs], qz[:, h, blk * P:(blk + 1) * P], kT[:, cs],
                                  start=True, stop=True)
                    last.then_inc(S["s2_ready"], 1)

                def transposed(w):
                    pe.wait_ge(S["p2_ready"], w + 1)
                    transpose_blocks(slot[t_slot(w)], ring[:, w % RING, :]).then_inc(S["t2_psum"], 1)

                def values(blk):
                    pe.wait_ge(S["t2_even"], H0 * (blk + 1))
                    pe.wait_ge(S["t2_odd"], H0 * (blk + 1))
                    for c in range(T):
                        for h in range(H0):
                            last = mm(acc[h * DH0:(h + 1) * DH0, blk // 4, blk % 4 * P:(blk % 4 + 1) * P],
                                      vn[:, c * P + h * DH0:c * P + (h + 1) * DH0], pT[:, h, c * P:(c + 1) * P],
                                      start=(c == 0), stop=(c == T - 1))
                    last.then_inc(S["pv2_done"], 1)

                scores(0)
                for w in range(UNITS2):
                    if w + 1 < UNITS2:
                        scores(w + 1)
                    if w == 0:
                        project_values(1)
                    if w == H0:
                        pe.wait_ge(S["v_ready"], 2)
                    if w and w % H0 == 0:
                        values(w // H0 - 1)
                    transposed(w)
                values(T - 1)
                for i in range(2):
                    pe.wait_ge(S["c2_ready"], i + 1)
                    transpose_half(slot[0], tA, i).then_inc(S["cn2_psum"], 1)
                for i in range(2):
                    pe.wait_ge(S["cn2_ready"], i + 1)
                    transpose_half(slot[1], tB, i).then_inc(S["cT2_psum"], 1)
                for i in range(2):
                    pe.wait_ge(S["cT2_ready"], i + 1)
                    project_rows(slot[2], tC, wT[:, 4 + WO, :], i).then_inc(S["o2_psum"], 1)

            def layer3(b):
                for s, w, name in ((1, w3[:, P:P + H3], "d3_psum"), (2, w3s[:], "s3_psum")):
                    for i in range(NH):
                        cs = slice(i * HALF, (i + 1) * HALF)
                        pe.wait_ge(S["hT_ready"], 6 + i + 1)
                        last = mm(psum[0:H3, s, cs], w, hT[:, cs], start=True, stop=True)
                    last.then_inc(S[name], 1)
                for t in range(T):
                    if t == T // 2:
                        pe.wait_ge(S["dmax3_ready"], 1)
                    last = mm(psum[:, t // 4, t % 4 * 256:t % 4 * 256 + P + H3], hT[:, t * P:(t + 1) * P], w3[:],
                              start=True, stop=True)
                last.then_inc(S["v3_psum"], 1)
                mm(acc[:, 0, 0:H3], ones[0:H3, :], diag3[:], start=True, stop=True).then_inc(S["dmaxb3_psum"], 1)
                pe.wait_ge(S["s3_shifted"], 1)
                pe.wait_ge(S["v3_ready"], 1)
                for c in range(T):
                    last = mm(psum[:, 2, 0:H3 * SLOT3], ones[:], v3[:, c, :, :].rearrange("p h f -> p (h f)"),
                              start=(c == 0), stop=(c == T - 1))
                last.then_inc(S["sum3_psum"], 1)
                for n in range(CHUNKS3):
                    g, c = n // T, n % T
                    pe.wait_ge(S["p3_ready"], 4 * n + 4)
                    if n == T:
                        pe.wait_ge(S["o3_ready"], 1)
                    for i in range(NH):
                        for h in range(4):
                            last = mm(acc[32 * h:32 * h + 32, i, :], v3[:, c, 4 * g + h, :],
                                      ring3[(4 * n + h) % RING3][:, i * HALF:(i + 1) * HALF],
                                      start=(c == 0), stop=(c == T - 1))
                        if n == CHUNKS3 - 1 and i == 0:
                            last.then_inc(S["pv3_done"], 1)
                    last.then_inc(S["pv3_done"], 1)
                    if n == T:
                        transpose_blocks(slot[0], tA).then_inc(S["on3_psum"], 1)
                for i in range(2):
                    pe.wait_ge(S["o3_ready"], i + 2)
                    transpose_half(slot[1], tC, i).then_inc(S["on3_psum"], 1)
                for i in range(2):
                    pe.wait_ge(S["cn3_ready"], i + 1)
                    transpose_half(slot[2], cn3, i).then_inc(S["cT3_psum"], 1)
                for i in range(2):
                    pe.wait_ge(S["cT3_ready"], i + 1)
                    project_rows(slot[0], tA, wT[:, WOUT3, :], i).then_inc(S["o3_psum"], 1)

            pe.wait_ge(S["h_first"], 1)
            with pe.Fori(0, B) as b:
                h_transposed(0, hn)
                queries_keys(0, 0)
                layer0(b)
                h_transposed(1, hx)
                layer1(b)
                h_transposed(2, hx)
                queries_keys(2, 1)
                layer2(b)
                h_transposed(3, hx)
                layer3(b)
                end_graph(pe, "go_pe")

        @block.scalar
        def _(act):
            link = Links(act, S["act_setup_link"])
            go = nc.scalar.activation
            act.add_instruction(mybir.InstLoadActFuncSet(act_func_set_id=EXP_AND_LN, name=nc.get_next_instruction_name(),
                                                         engine=mybir.EngineType.Activation))

            act.wait_ge(S["wt_psum"], 1)
            go(wT[:, 0:8, :].rearrange("p w o -> p (w o)"), slot[0], ACT.Copy)
            go(wT[:, 8, :], slot[1][:, 0:P], ACT.Copy).then_inc(S["wt_copied"], 1)
            act.wait_ge(S["weights_in"], n_weights)
            act.wait_ge(S["beta_e"], 1)
            link(go(beta3[:, 1:2], beta3[:, 1:2], ACT.Exp, scale=-1.0))
            go(beta3[:, 1:2], beta3[:, 1:2], ACT.Ln, bias=1.0).then_inc(S["beta_ready"], 1)
            act.wait_ge(S["beta_e"], 2)
            act.wait_ge(S["adjf"], 2)
            for c in range(T):
                act.wait_ge(S["g_lin"], c + 1)
                link(go(prior[:, c, :], prior[:, c, :], ACT.Ln, scale=amax[:, 3:4], bias=amax[:, 4:5]))
                go(prior[:, c, :], prior[:, c, :], ACT.Exp, scale=beta3[:, 2:3]).then_inc(S["g_log"], 1)

            isds = [0]

            def inverse_deviation(halves, first=False):
                ts = slice(0, T) if halves is None else slice(halves * T // 2, (halves + 1) * T // 2)
                if not first:
                    isds[0] += 1
                act.wait_ge(S["var_first" if first else "var_ready"], 1 if first else isds[0])
                link(go(lnv[:, ts], veps[:, ts], ACT.Ln))
                go(isd[:, ts], lnv[:, ts], ACT.Exp, scale=-0.5).then_inc(S["isd_first" if first else "isd_ready"], 1)

            def h_transposed(layer):
                for i in range(2):
                    act.wait_ge(S["hT_psum"], 2 * layer + i + 1)
                    cs = slice(i * HALF, (i + 1) * HALF)
                    go(hT[:, cs], slot[0][:, cs], ACT.Relu).then_inc(S["hT_ready"], 1)

            def spread_q(k):
                act.wait_ge(S["q_psum"], k + 1)
                act.wait_ge(S["qz_zero"], 1)
                for h in range(H0 - 1):
                    ps = slice(h * DH0, (h + 1) * DH0)
                    go(qz[ps, h, :], psum[ps, 1, :], ACT.Identity,
                       bias=cols[ps, 2 * k:2 * k + 1]).then_inc(S["qz_ready"], 1)

            def layer0(b):
                def weights(u):
                    act.wait_ge(S["s0_ready"], u + 1)
                    if u >= RING:
                        act.wait_ge(S["pv0_done"], (u - RING) // 2 + 1)
                    go(ring[:, u % RING, :], slot[slot0(u)], ACT.Exp, scale=SCALE).then_inc(S["e0_done"], 1)

                def inverse_sums(m):
                    act.wait_ge(S["pv0_done"], m + 1)
                    if m >= 2:
                        act.wait_ge(S["ctx0_read"], m - 1)
                    go(rzs[:, m % 2, :], acc[:, 1, :], ACT.Ln).then_inc(S["z0_read"], 1)
                    act.wait_ge(S["z0_read"], m + 1)
                    go(rzs[:, m % 2, :], rzs[:, m % 2, :], ACT.Exp, scale=-1.0).then_inc(S["rz0_ready"], 1)

                for n in range(CHUNKS0):
                    if n >= 2:
                        inverse_sums(n - 2)
                    weights(2 * n)
                    if n in (O0_AT // 2 + 1, O0_AT // 2 + 2):
                        inverse_deviation(0)
                    weights(2 * n + 1)
                inverse_sums(CHUNKS0 - 2)
                inverse_sums(CHUNKS0 - 1)

            def layer1(b):
                act.wait_ge(S["s1_shifted"], 1)
                go(tB[:], tA[:], ACT.Exp, scale=-(1 - ALPHA)).then_inc(S["r1_ready"], 1)
                act.wait_ge(S["dm1_ready"], 1)
                go(b1, dm1, ACT.Exp)
                go(d1, dm1, ACT.Exp, scale=ALPHA).then_inc(S["b1_ready"], 1)
                act.wait_ge(S["nb1_ready"], 1)
                act.wait_ge(S["r1_ready"], 1)
                act.wait_ge(S["b1_ready"], 1)
                for c in range(T):
                    if c >= RING:
                        act.wait_ge(S["pv1_done"], c - RING + 1)
                        act.wait_ge(S["z1_done"], 1)
                    go(ring[:, c % RING, :], tB[:], ACT.Relu, scale=d1[:, c:c + 1],
                       bias=nb1[:, c:c + 1]).then_inc(S["t1_ready"], 1)
                for i in range(2):
                    cs = slice(i * HALF, (i + 1) * HALF)
                    act.wait_ge(S["pv1_done"], T + i)
                    go(tA[:, cs], acc[:, i, :], ACT.Copy).then_inc(S["u1_ready"], 1)
                for i in range(2):
                    cs = slice(i * HALF, (i + 1) * HALF)
                    act.wait_ge(S["neg1_ready"], i + 1)
                    go(tC[:, cs], tC[:, cs], ACT.Exp).then_inc(S["e1_ready"], 1)

            def layer2(b):
                def weights(w):
                    act.wait_ge(S["nm2_ready"], w + 1)
                    if w >= RING:
                        act.wait_ge(S["t2_psum"], w - RING + 1)
                    go(ring[:, w % RING, :], slot[0 if w == 0 else (2 * w - 1) % 3], ACT.Exp, scale=-1.0,
                       bias=nm2[:, w:w + 1], accum_out=z2[:, w:w + 1]).then_inc(S["p2_ready"], 1)

                def copy_odd(w):
                    act.wait_ge(S["t2_psum"], w + 1)
                    if w >= H0:
                        act.wait_ge(S["pv2_done"], w // H0)
                    go(pT[:, w % H0, HALF:N], psum[:, (2 * w + 2) % 3, HALF:N], ACT.Copy).then_inc(S["t2_odd"], 1)

                def context(i):
                    act.wait_ge(S["pv2_done"], (i + 1) * T // 2)
                    go(tA[:, i * HALF:(i + 1) * HALF], acc[:, i, :], ACT.Copy).then_inc(S["c2_ready"], 1)

                for w in range(UNITS2):
                    weights(w)
                    if w:
                        copy_odd(w - 1)
                    if w == NEXT_NORM_AT + 2:
                        inverse_deviation(None)
                    if w == UNITS2 // 2 + 4:
                        context(0)
                copy_odd(UNITS2 - 1)
                context(1)
                for i in range(2):
                    cs = slice(i * HALF, (i + 1) * HALF)
                    act.wait_ge(S["cn2_ready"], 2)
                    act.wait_ge(S["cT2_psum"], i + 1)
                    go(tC[:, cs], slot[1][:, cs], ACT.Copy).then_inc(S["cT2_ready"], 1)

            def layer3(b):
                act.wait_ge(S["s3_shifted"], 1)
                go(tB[0:H3, :], tA[0:H3, :], ACT.Exp, scale=-(1 - ALPHA)).then_inc(S["r3_ready"], 1)
                act.wait_ge(S["dm3_ready"], 1)
                go(b3, dm3, ACT.Exp)
                go(d3, dm3, ACT.Exp, scale=ALPHA).then_inc(S["b3_ready"], 1)
                act.wait_ge(S["nb3_ready"], 1)
                act.wait_ge(S["b3_ready"], 1)
                for v in range(UNITS3):
                    g, c, h = v // (4 * T), v // 4 % T, v // (4 * T) * 4 + v % 4
                    if c == 0:
                        act.wait_ge(S[f"r3_in{h}"], 16)
                    if v == 4 * T + 4:
                        act.wait_ge(S["pv3_done"], T)
                        go(tA[:], acc[:].rearrange("p i c -> p (i c)"), ACT.Copy).then_inc(S["o3_ready"], 1)
                    if v >= RING3:
                        act.wait_ge(S["pv3_done"], (v - RING3) // 4 + 1)
                    fac = pT[:, h, :] if g == 0 else qz[:, h - 4, :]
                    go(ring3[v % RING3], fac, ACT.Relu, scale=d3[:, c, h:h + 1],
                       bias=nb3[:, c, h:h + 1]).then_inc(S["t3_ready"], 1)
                for i in range(2):
                    act.wait_ge(S["pv3_done"], CHUNKS3 + i)
                    go(tC[:, i * HALF:(i + 1) * HALF], acc[:, i, :], ACT.Copy).then_inc(S["o3_ready"], 1)
                for i in range(2):
                    cs = slice(i * HALF, (i + 1) * HALF)
                    act.wait_ge(S["cT3_psum"], i + 1)
                    go(tA[:, cs], slot[2][:, cs], ACT.Copy).then_inc(S["cT3_ready"], 1)

            inverse_deviation(None, first=True)
            link = Links(act, S["act_link"])
            with act.Fori(0, B) as b:
                h_transposed(0)
                spread_q(0)
                layer0(b)
                inverse_deviation(1)
                inverse_deviation(1)
                h_transposed(1)
                layer1(b)
                inverse_deviation(0)
                inverse_deviation(1)
                h_transposed(2)
                spread_q(1)
                layer2(b)
                inverse_deviation(0)
                inverse_deviation(1)
                h_transposed(3)
                layer3(b)
                end_graph(act, "go_act")

        @block.vector
        def _(v):
            link = Links(v, S["dve_setup_link"])

            af = ring[:, 0:T, :]
            v.wait_ge(S["adj_in"], 16)
            link(v.tensor_copy(af, prior[:].bitcast(I32)))
            link(v.tensor_reduce(rowmax[:], af, AX.X, ALU.max))
            v.tensor_reduce(amax[:, 0:1], rowmax[:], AX.X, ALU.max).then_inc(S["amax_t"], 1)
            v.tensor_scalar(maskN[:], af, 0.0, -BIG, ALU.is_equal, ALU.mult)
            v.tensor_scalar(empty3[:], rowmax[:], 0.0, None, ALU.is_le)
            v.wait_ge(S["weights_in"], n_weights)
            link(v.tensor_tensor(tA[:, 0:P], w1[:, 0:P], a1b[:, 0:P], ALU.mult))
            v.tensor_tensor(tA[:, P:2 * P], w1[:, 0:P], a1b[:, P:2 * P], ALU.mult)
            v.tensor_tensor(tB[:, 0:P], w3[:, 0:P], a3b[:, 0, :], ALU.mult)
            link(v.tensor_tensor(tB[:, P:2 * P], w3[:, 0:P], a3b[:, 1, :], ALU.mult))
            v.tensor_reduce(wa1[:], tA[:, 0:2 * P].rearrange("p (k o) -> p k o", k=2), AX.X, ALU.add)
            v.tensor_reduce(w3s[:], tB[:, 0:P].rearrange("p (h f) -> p h f", h=H3), AX.X, ALU.add)
            link(v.tensor_reduce(w3[:, P:P + H3], tB[:, P:2 * P].rearrange("p (h f) -> p h f", h=H3), AX.X, ALU.add))
            v.wait_ge(S["consts"], 1)
            v.tensor_copy(w1[:, P:P + 1], wa1[:, 1:2])
            v.tensor_scalar(w1s[:], ones[:], wa1[:, 0:1], None, ALU.mult)
            v.tensor_scalar(w1d[:], ones[:], wa1[:, 1:2], None, ALU.mult).then_inc(S["wa_ready"], 1)
            link(v.tensor_scalar(beta3[:, 1:2], beta3[:, 0:1], -1.0, None, ALU.mult))
            v.tensor_scalar(beta3[:, 3:4], beta3[:, 0:1], 0.0, None, ALU.max)
            link(v.tensor_tensor(beta3[:, 1:2], beta3[:, 1:2], beta3[:, 0:1], ALU.max))
            v.sem_inc(S["beta_e"], 1)
            v.wait_ge(S["beta_ready"], 1)
            v.tensor_tensor(beta3[:, 2:3], beta3[:, 1:2], beta3[:, 3:4], ALU.add).then_inc(S["beta_e"], 1)
            v.wait_ge(S["amax_tr"], 1)
            v.tensor_reduce(amax[0:1, 1:2], acc[0:1, 0, 0:P], AX.X, ALU.max).then_inc(S["amax_row"], 1)
            v.wait_ge(S["amax_b"], 1)
            link(v.tensor_scalar(amax[:, 2:3], acc[:, 1, 0:1], 0.0, PRIOR_EPS, ALU.max, ALU.add))
            link(v.reciprocal(amax[:, 3:4], amax[:, 2:3]))
            link(v.tensor_scalar(amax[:, 4:5], amax[:, 3:4], PRIOR_EPS, None, ALU.mult))
            v.sem_inc(S["adjf"], 2)
            for c in range(T):
                v.wait_ge(S["adjT_psum"], c + 1)
                v.tensor_scalar(prior[:, c, :], slot[c % 3], 0.0, None, ALU.max).then_inc(S["g_lin"], 1)
                v.tensor_scalar(mask1[:, c, :], slot[c % 3], 0.0, None, ALU.is_gt)
                link(v.tensor_scalar(clipU[:, c, :], slot[c % 3], 0.0, E_HI, ALU.not_equal, ALU.mult))
                v.sem_inc(S["adjT_read"], 1)
                v.tensor_scalar(clipU[:, c, :], clipU[:, c, :], E_LO, None, ALU.max)
            for c in range(T):
                v.wait_ge(S["g_log"], c + 1)
                last = v.tensor_tensor(prior[:, c, :], prior[:, c, :], mask1[:, c, :], ALU.mult)
            link(last)

            isds = [0]

            def half_blocks(i):
                return range(T) if i is None else range(i * T // 2, (i + 1) * T // 2)

            def norm_stats(i, src, first=False):
                ts = half_blocks(i)
                for t in ts:
                    last = v.bn_stats(bnst[:, t, :], src[:, t * P:(t + 1) * P])
                link(last)
                for t in ts:
                    last = v.bn_aggr(mv[:, t, :], bnst[:, t, :])
                link(last)
                cs = slice(ts[0], ts[-1] + 1)
                v.tensor_scalar(veps[:, cs], mv[:, cs, 1], LN_EPS, None,
                                ALU.add).then_inc(S["var_first" if first else "var_ready"], 1)

            def norm_apply(i, dst, src, first=False):
                ts = half_blocks(i)
                cs = slice(ts[0], ts[-1] + 1)
                if not first:
                    isds[0] += 1
                v.wait_ge(S["isd_first" if first else "isd_ready"], 1 if first else isds[0])
                link(v.tensor_tensor(nwt[:, cs], isd[:, cs], isd[:, cs], ALU.mult))
                link(v.scalar_tensor_tensor(out=nwt[:, cs], in0=nwt[:, cs], scalar=-0.5, in1=veps[:, cs],
                                            op0=ALU.mult, op1=ALU.mult))
                link(v.scalar_tensor_tensor(out=rstd[:, cs], in0=nwt[:, cs], scalar=1.5, in1=isd[:, cs],
                                            op0=ALU.add, op1=ALU.mult))
                for t in ts:
                    bs = slice(t * P, (t + 1) * P)
                    last = v.tensor_scalar(dst[:, bs], src[:, bs], mv[:, t, 0:1], rstd[:, t:t + 1],
                                           ALU.subtract, ALU.mult)
                return last

            def pre_norm_apply():
                for i in range(2):
                    norm_apply(i, hx, xs).then_inc(S["h_ready"], 1)

            def queries_keys(k):
                v.wait_ge(S["k_psum"], k + 1)
                v.tensor_scalar(kT[:], slot[2], cols[:, 2 * k + 1:2 * k + 2], None, ALU.add).then_inc(S["kT_ready"], 1)
                ps = slice((H0 - 1) * DH0, P)
                v.wait_ge(S["q_psum"], k + 1)
                v.wait_ge(S["qz_zero"], 1)
                v.tensor_scalar(qz[ps, H0 - 1, :], psum[ps, 1, :], cols[ps, 2 * k:2 * k + 1], None,
                                ALU.add).then_inc(S["qz3_ready"], 1)

            def values(k):
                v.wait_ge(S["v_psum"], k + 1)
                v.tensor_tensor(blocks(vn[:]), blocks(acc[:].rearrange("p i c -> p (i c)")),
                                repeat(rows[:, (BV0, BV2)[k], :], T), ALU.add).then_inc(S["v_ready"], 1)

            def layer0(b):
                adds = CHUNKS0 - NH
                v.wait_ge(S["x_stored"], 16)
                v.sem_clear(S["x_stored"])

                def clip(u):
                    n = u // 2
                    half, c = n // T, n % T
                    v.wait_ge(S["e0_done"], u + 1)
                    tile = ring[:, u % RING, :].rearrange("p (i c) -> p i c", i=2)
                    v.scalar_tensor_tensor(out=tile, in0=tile, scalar=E_LO,
                                           in1=repeat(clipU[:, c, half * HALF:(half + 1) * HALF], 2),
                                           op0=ALU.max, op1=ALU.min).then_inc(S["p0_ready"], 1)

                def scale(m):
                    v.wait_ge(S["rz0_ready"], m + 1)
                    half = slice(m // T * HALF, (m // T + 1) * HALF)
                    if m % T and m >= 2 and (m - 2) % T:
                        v.wait_ge(S["ctx0_added"], (m - 2) - (m - 2) // T)
                    dst = part0[:, m % 2, :] if m % T else ctx0[:, half]
                    v.tensor_tensor(dst, acc[:, 0, :], rzs[:, m % 2, :], ALU.mult).then_inc(S["ctx0_read"], 1)

                def residual(i):
                    cs = slice(i * HALF, (i + 1) * HALF)
                    v.wait_ge(S["biased"], 1)
                    v.wait_ge(S["o0_psum"], i + 1)
                    link(v.tensor_tensor(tA[:, cs], slot[O0_AT % 3 if i == 0 else 0][:, cs], hn[:, cs], ALU.add))
                    v.sem_inc(S["o0_read"], 1)
                    norm_stats(i, tA)

                def finish(i):
                    cs = slice(i * HALF, (i + 1) * HALF)
                    link(norm_apply(i, tA, tA))
                    link(v.tensor_tensor(blocks(tA[:, cs]), blocks(tA[:, cs]), repeat(rows[:, GAMMA, :], T // 2),
                                         ALU.mult))
                    link(v.tensor_tensor(xs[:, cs], xin[:, cs], tA[:, cs], ALU.add))
                    norm_stats(i, xs)

                for n in range(CHUNKS0):
                    if n >= 2:
                        scale(n - 2)
                    clip(2 * n)
                    clip(2 * n + 1)
                    if n == 0:
                        values(0)
                    if n == O0_AT // 2:
                        residual(0)
                    if n == O0_AT // 2 + 1:
                        finish(0)
                    if n == O0_AT // 2 + 2:
                        norm_apply(0, hx, xs).then_inc(S["h_ready"], 1)
                scale(CHUNKS0 - 2)
                scale(CHUNKS0 - 1)
                residual(1)
                finish(1)
                v.sem_inc(S["xin_used"], 1)
                norm_apply(1, hx, xs).then_inc(S["h_ready"], 1)

            def layer1(b):
                v.wait_ge(S["d1_psum"], 1)
                link(v.tensor_reduce(dmax1[:], slot[1], AX.X, ALU.max))
                v.sem_inc(S["dmax1_ready"], 1)
                v.wait_ge(S["s1_psum"], 1)
                v.tensor_scalar(tA[:], slot[2], dmax1[:, 0:1], -100.0, ALU.add, ALU.max).then_inc(S["s1_shifted"], 1)
                v.wait_ge(S["v1_psum"], 1)
                view = psum[:, 0:2, :].rearrange("p s (k c) -> p (s k) c", c=256)
                v.tensor_scalar(dm1, view[:, :, P], dmax1[:, 0:1], None, ALU.subtract).then_inc(S["dm1_ready"], 1)
                v.tensor_copy(blocks(vn[:]), view[:, :, 0:P]).then_inc(S["v1_ready"], 1)
                v.wait_ge(S["b1_ready"], 1)
                v.tensor_scalar(nb1, b1, -1.0, None, ALU.mult).then_inc(S["nb1_ready"], 1)
                for c in range(T):
                    v.wait_ge(S["t1_ready"], c + 1)
                    v.scalar_tensor_tensor(out=ring[:, c % RING, :], in0=ring[:, c % RING, :], scalar=b1[:, c:c + 1],
                                           in1=mask1[:, c, :], op0=ALU.add, op1=ALU.mult).then_inc(S["p1_ready"], 1)
                v.wait_ge(S["z1_done"], 2)
                v.tensor_copy(tC[:], slot[2]).then_inc(S["zc1_ready"], 1)
                for i in range(2):
                    cs, ts = slice(i * HALF, (i + 1) * HALF), slice(i * T // 2, (i + 1) * T // 2)
                    v.wait_ge(S["n1_psum"], i + 1)
                    link(v.reciprocal(rz1[:, ts], slot[1][:, ts]))
                    link(v.tensor_tensor(blocks(tA[:, cs]), blocks(slot[0][:, cs]), spread(rz1[:, ts], P), ALU.mult))
                    v.tensor_scalar(tC[:, cs], tA[:, cs], 0.0, None, ALU.min).then_inc(S["neg1_ready"], 1)
                    link(v.tensor_scalar(tA[:, cs], tA[:, cs], 0.0, None, ALU.max))
                for i in range(2):
                    cs = slice(i * HALF, (i + 1) * HALF)
                    v.wait_ge(S["e1_ready"], i + 1)
                    link(v.scalar_tensor_tensor(out=tA[:, cs], in0=tC[:, cs], scalar=-1.0, in1=tA[:, cs],
                                                op0=ALU.add, op1=ALU.add))
                    link(v.tensor_tensor(xs[:, cs], xs[:, cs], tA[:, cs], ALU.add))
                    norm_stats(i, xs)
                pre_norm_apply()

            def layer2(b):
                def row_max(w):
                    v.wait_ge(S["s2_ready"], w + 1)
                    tile = slot[0 if w == 0 else (2 * w - 1) % 3]
                    v.tensor_tensor_reduce(out=tile, in0=tile, in1=maskN[:, w // H0, :], scale=-SCALE, scalar=-FLOOR,
                                           op0=ALU.add, op1=ALU.min,
                                           accum_out=nm2[:, w:w + 1]).then_inc(S["nm2_ready"], 1)

                def copy_even(w):
                    v.wait_ge(S["t2_psum"], w + 1)
                    if w >= H0:
                        v.wait_ge(S["pv2_done"], w // H0)
                    v.tensor_copy(pT[:, w % H0, 0:HALF], psum[:, (2 * w + 2) % 3, 0:HALF]).then_inc(S["t2_even"], 1)

                for w in range(UNITS2):
                    row_max(w)
                    if w == 1:
                        values(1)
                    if w:
                        copy_even(w - 1)
                    if w == NEXT_NORM_AT:
                        v.wait_ge(S["x_in"], 16)
                        v.sem_clear(S["x_in"])
                        norm_stats(None, xin)
                    if w == NEXT_NORM_AT + 4:
                        norm_apply(None, hn, xin)
                copy_even(UNITS2 - 1)
                v.wait_ge(S["p2_ready"], UNITS2)
                link(v.tensor_scalar(z2, z2, 1e-30, None, ALU.max))
                link(v.reciprocal(rz2, z2))
                for i in range(2):
                    cs, ws = slice(i * HALF, (i + 1) * HALF), slice(i * UNITS2 // 2, (i + 1) * UNITS2 // 2)
                    v.wait_ge(S["cn2_psum"], i + 1)
                    v.tensor_tensor(tB[:, cs].rearrange("p (w d) -> p w d", d=DH0),
                                    slot[0][:, cs].rearrange("p (w d) -> p w d", d=DH0), spread(rz2[:, ws], DH0),
                                    ALU.mult).then_inc(S["cn2_ready"], 1)
                v.wait_ge(S["biased"], 2)
                for i in range(2):
                    cs = slice(i * HALF, (i + 1) * HALF)
                    v.wait_ge(S["o2_psum"], i + 1)
                    link(v.tensor_tensor(xs[:, cs], xs[:, cs], slot[2][:, cs], ALU.add))
                    norm_stats(i, xs)
                pre_norm_apply()

            def layer3(b):
                v.wait_ge(S["d3_psum"], 1)
                link(v.tensor_reduce(dmax3[:], psum[0:H3, 1, :], AX.X, ALU.max))
                v.tensor_scalar(diag3[:], ident[0:H3, 0:H3], dmax3[:, 0:1], None, ALU.mult).then_inc(S["dmax3_ready"], 1)
                v.wait_ge(S["s3_psum"], 1)
                v.tensor_scalar(tA[0:H3, :], psum[0:H3, 2, :], dmax3[:, 0:1], -100.0, ALU.add,
                                ALU.max).then_inc(S["s3_shifted"], 1)
                v.wait_ge(S["v3_psum"], 1)
                view = psum[:, 0:2, :].rearrange("p s (k c) -> p (s k) c", c=256)
                v.tensor_copy(v3[:, :, :, 0:DH3], view[:, :, 0:P].rearrange("p t (h f) -> p t h f", h=H3)).then_inc(S["v3_ready"], 1)
                v.wait_ge(S["dmaxb3_psum"], 1)
                link(v.tensor_copy(dmaxb3[:], acc[:, 0, 0:H3]))
                v.tensor_tensor(dm3, view[:, :, P:P + H3], repeat(dmaxb3[:], T), ALU.subtract).then_inc(S["dm3_ready"], 1)
                v.wait_ge(S["b3_ready"], 1)
                v.tensor_scalar(nb3, b3, -1.0, None, ALU.mult).then_inc(S["nb3_ready"], 1)
                v.wait_ge(S["sum3_psum"], 1)
                link(v.tensor_copy(sv3, psum[:, 2, 0:H3 * SLOT3]))

                def normalise(g, i):
                    ts = half_blocks(i)
                    for t in ts:
                        last = v.scalar_tensor_tensor(out=tB[:, t * P:(t + 1) * P], in0=sv3[:, g * P:(g + 1) * P],
                                                      scalar=empty3[:, t:t + 1], in1=slot[g][:, t * P:(t + 1) * P],
                                                      op0=ALU.mult, op1=ALU.add)
                    link(last)
                    nat = tB[:].rearrange("p (w c) -> p w c", c=SLOT3)
                    ws = slice(4 * ts[0], 4 * ts[-1] + 4)
                    link(v.reciprocal(rz3[:, g, ws], nat[:, ws, DH3]))
                    for t in ts:
                        last = v.tensor_tensor(
                            cn3[:, t * P + g * 64:t * P + g * 64 + 64].rearrange("p (h f) -> p h f", h=4),
                            nat[:, 4 * t:4 * t + 4, 0:DH3], spread(rz3[:, g, 4 * t:4 * t + 4], DH3), ALU.mult)
                    return last

                for u in range(UNITS3):
                    g, c, h = u // (4 * T), u // 4 % T, u // (4 * T) * 4 + u % 4
                    v.wait_ge(S["t3_ready"], u + 1)
                    v.scalar_tensor_tensor(out=ring3[u % RING3], in0=ring3[u % RING3], scalar=b3[:, c, h:h + 1],
                                           in1=prior[:, c, :], op0=ALU.add, op1=ALU.mult).then_inc(S["p3_ready"], 1)
                    if u == 4 * T + 12:
                        v.wait_ge(S["on3_psum"], 1)
                        link(normalise(0, None))
                for i in range(2):
                    v.wait_ge(S["on3_psum"], i + 2)
                    normalise(1, i).then_inc(S["cn3_ready"], 1)
                for i in range(2):
                    cs = slice(i * HALF, (i + 1) * HALF)
                    v.wait_ge(S["o3_psum"], i + 1)
                    last = v.tensor_tensor(xs[:, cs], xs[:, cs], slot[0][:, cs], ALU.add)
                link(last)
                v.sem_inc(S["x_done"], 1)

            v.wait_ge(S["x_in"], 16)
            v.sem_clear(S["x_in"])
            norm_stats(None, xin, first=True)
            norm_apply(None, hn, xin, first=True).then_inc(S["h_first"], 1)
            link = Links(v, S["dve_link"])
            with v.Fori(0, B) as b:
                queries_keys(0)
                layer0(b)
                layer1(b)
                queries_keys(1)
                layer2(b)
                layer3(b)
                end_graph(v, "go_v")


def kernel(**inputs):
    import concourse.bacc as bacc
    from concourse.bass_utils import run_bass_kernel_spmd

    nc = bacc.Bacc("TRN2", target_bir_lowering=False, num_devices=1)
    arrays, aps = {}, {}
    for name in INPUTS:
        arr = np.ascontiguousarray(inputs[name])
        if arr.ndim == 0:
            arr = arr.reshape(1, 1)
        arrays[f"in_{name}"] = arr
        aps[name] = nc.dram_tensor(f"in_{name}", arr.shape, mybir.dt.from_np(arr.dtype), kind="ExternalInput").ap()
    scratch = nc.dram_tensor("row_factors", (H3, N), F32).ap()
    out = nc.dram_tensor("out_0", (B, N, D), F32, kind="ExternalOutput").ap()
    build(nc, aps, scratch, out)
    r = run_bass_kernel_spmd(nc, [arrays], core_ids=[0])
    return r.results[0]["out_0"]
```

```python
from contextlib import ExitStack

import numpy as np

import concourse.bass as bass
from concourse import mybir

F32 = mybir.dt.float32
BF16 = mybir.dt.bfloat16
I32 = mybir.dt.int32
ACT = mybir.ActivationFunctionType
ALU = mybir.AluOpType
AX = mybir.AxisListType

P = 128
B, N, D = 8, 1024, 128
T = N // P
HALF = 512
NH = N // HALF
H0, DH0 = 4, 32
H3, DH3 = 8, 16
SLOT3 = 32
RING = 6
SCALE = 1.0 / float(np.sqrt(DH0))
E_HI, E_LO = float(np.exp(10.0)), float(np.exp(-10.0))
BIG = 1e38
FLOOR = -1e30
ALPHA = 0.2
PRIOR_EPS = 1e-6
LN_EPS = 1e-5
EXP_AND_LN = 6
UNITS0 = 2 * NH * T
CHUNKS0 = NH * T
O0_AT = 24
NEXT_NORM_AT = 8
UNITS2 = T * H0
UNITS3 = H3 * T
CHUNKS3 = UNITS3 // 4

INPUTS = ["x", "adj", "L0_gnn_Wq", "L0_gnn_bq", "L0_gnn_Wk", "L0_gnn_bk", "L0_gnn_Wv", "L0_gnn_bv",
          "L0_gnn_Wo", "L0_gnn_bo", "L0_gnn_gamma", "L0_gnn_beta", "L1_gnn_W", "L1_gnn_a",
          "L2_gnn_wq", "L2_gnn_bq", "L2_gnn_wk", "L2_gnn_bk", "L2_gnn_wv", "L2_gnn_bv", "L2_gnn_wo",
          "L2_gnn_bo", "L3_gnn_W", "L3_gnn_a_src", "L3_gnn_a_dst", "L3_gnn_beta_tilde", "L3_gnn_W_out"]

SQUARE = ["L0_gnn_Wq", "L0_gnn_Wk", "L0_gnn_Wv", "L0_gnn_Wo", "L2_gnn_wq", "L2_gnn_wk", "L2_gnn_wv",
          "L2_gnn_wo", "L3_gnn_W_out"]
WQ, WK, WV, WO = 0, 1, 2, 3
WOUT3 = 8
COLS = ["L0_gnn_bq", "L0_gnn_bk", "L2_gnn_bq", "L2_gnn_bk"]
ROWS = ["L0_gnn_bv", "L0_gnn_bo", "L0_gnn_gamma", "L0_gnn_beta", "L2_gnn_bv", "L2_gnn_bo"]
BV0, BO0, GAMMA, BETA, BV2, BO2 = range(6)



class Links:

    def __init__(self, eng, sem):
        self.eng, self.sem, self.n = eng, sem, 0

    def __call__(self, ins):
        self.n += 1
        ins.then_inc(self.sem, 1)
        self.eng.wait_ge(self.sem, self.n)


def blocks(ap):
    return ap.rearrange("p (t d) -> p t d", d=P)


def spread(ap, n):
    return ap.unsqueeze(2).broadcast_to((ap.shape[0], ap.shape[1], n))


def repeat(ap, n):
    return ap.unsqueeze(1).broadcast_to((ap.shape[0], n, ap.shape[1]))


def build(nc, a, out):
    with ExitStack() as ctx:
        def sb(name, shape, dt=F32):
            return ctx.enter_context(nc.sbuf_tensor(name, shape, dt))

        def sem(name):
            return ctx.enter_context(nc.semaphore(name))

        clipU = sb("clipU", [P, T, N])
        prior = sb("prior", [P, T, N])
        mask1 = sb("mask1", [P, T, N], BF16)
        maskN = sb("maskN", [P, T, N], BF16)
        wT = sb("wT", [P, len(SQUARE), P])
        w1 = sb("w1", [P, P + 1])
        w3 = sb("w3", [P, P + H3])
        w3s = sb("w3s", [P, H3])
        w3w = sb("w3w", [P, 2, P])
        cols = sb("cols", [P, len(COLS)])
        rows = sb("rows", [P, len(ROWS), P])
        wa1 = sb("wa1", [P, 2])
        ident = sb("ident", [P, P])
        ones = sb("ones", [P, P])
        beta3 = sb("beta3", [P, 4])
        rowmax = sb("rowmax", [P, T])
        empty3 = sb("empty3", [P, T])
        amax = sb("amax", [P, 8])
        xin = sb("xin", [P, N])
        xs = sb("xs", [P, N])
        hn = sb("hn", [P, N])
        hT = sb("hT", [P, N])
        qz = sb("qz", [P, H0, N])
        kT = sb("kT", [P, N])
        vn = sb("vn", [P, N])
        ring = sb("ring", [P, RING + H0, N])
        pT = ring[:, RING:RING + H0, :]
        fac3 = {3: pT[:, 3, :], 7: pT[:, 2, :], 6: pT[:, 1, :]}
        RING3 = RING + 2
        tA, tB, tC = (sb(n, [P, N]) for n in ("tA", "tB", "tC"))
        a1b = tC[:, 0:2 * P]
        a3b = tC[:, 2 * P:4 * P].rearrange("p (k c) -> p k c", k=2)
        cn3 = pT[:, 0, :]
        ring3 = [ring[:, i, :] for i in range(RING)] + [hT[:], tC[:]]
        v3 = sb("v3", [P, T, H3, SLOT3])
        bnst = sb("bnst", [P, T, 6])
        mv = sb("mv", [P, T, 2])
        veps, lnv, isd, nwt, rstd = (sb(n, [P, T]) for n in ("veps", "lnv", "isd", "nwt", "rstd"))
        dmax1 = sb("dmax1", [P, 1])
        dm1, c1, d1, rz1 = (kT[:, i * T:(i + 1) * T] for i in range(4))
        v1 = pT[:, 0:2, :].rearrange("p a (t c) -> p (a t) c", c=256)
        tiles1 = [ring[:, i, :] for i in range(RING)] + [pT[:, 2, :], vn[:]]
        nm2, z2, rz2 = (tC[:, i * UNITS2:(i + 1) * UNITS2] for i in range(3))
        dmax3 = sb("dmax3", [P, 1])
        diag3 = sb("diag3", [P, H3])
        hsum = sb("hsum", [P, NH])
        dmaxb3 = sb("dmaxb3", [P, H3])
        sv3 = vn[:, 0:H3 * SLOT3]
        dm3, c3, d3, nc3, rz3 = (vn[:, HALF // 2 + i * T * H3:HALF // 2 + (i + 1) * T * H3] for i in range(5))
        dm3, c3, d3, nc3 = (t.rearrange("p (t h) -> p t h", h=H3) for t in (dm3, c3, d3, nc3))
        rz3 = rz3.rearrange("p (g w) -> p g w", g=2)

        psum = ctx.enter_context(nc.psum_tensor("psum", [P, 3, N], F32))
        acc = ctx.enter_context(nc.psum_tensor("acc", [P, NH, HALF], F32))
        def slot0(u):
            return (u if u < O0_AT else u + 1) % 3

        slot = [psum[:, i, :] for i in range(3)]
        hT0 = pT[:, 3, :]
        sums1 = [slot[2].rearrange("p (t c) -> p t c", c=256), acc[:].rearrange("p i (t c) -> p (i t) c", c=256)]
        hx = pT[:, 3, :]
        rzs = tB[:].rearrange("p (r c) -> p r c", r=2)
        part0 = tC[:].rearrange("p (r c) -> p r c", r=2)
        ctx0 = xs

        S = {n: sem(n) for n in """weights_in adj_in x_in x_stored go_pe go_act go_v go_pool consts wt_psum wt_copied wa_ready
             amax_t amax_tr amax_row amax_b af_ready af_used adjf adjT_psum adjT_read adjT_taken g_log beta_e beta_ready
             dve_setup_link act_setup_link qz_zero var_first isd_first h_first first_hT_psum first_hT first_k_psum first_kT first_q_psum first_q pool_link""".split()}
        per_graph = {n: sem(n) for n in """var_ready isd_ready h_ready hT_psum hT_ready xin_used
             q_psum k_psum v_psum qz_ready qz3_ready kT_ready v_ready
             s0_ready e0_done p0_ready pv0_done z0_read rz0_ready ctx0_read ctx0_added o0_psum o0_read
             d1_psum s1_psum v1_psum dmax1_ready s1_shifted dm1_ready r1_ready c1_ready
             p1_ready n1_psum neg1_ready e1_ready
             s2_ready nm2_ready p2_ready t2_psum t2_even t2_odd pv2_done c2_ready cn2_psum cn2_ready
             cT2_psum cT2_ready o2_psum
             d3_psum s3_psum v3_psum dmax3_ready s3_shifted r3_ready r3_psum fac3_ready v3_ready sums3_read
             dmaxb3_psum dm3_ready c3_ready nc3_ready t3_ready p3_ready p3_pool slot2_read next_hT_psum next_hT next_k_psum next_kT next_q_psum next_q pv3_done o3_ready
             on3_psum cn3_ready cT3_psum cT3_ready o3_psum x_done turn_over biased pool_graph_link dve_link act_link""".split()}
        S.update(per_graph)
        numbers = sorted(s.num for s in per_graph.values())
        assert numbers == list(range(numbers[0], numbers[-1] + 1))
        block = ctx.enter_context(nc.Block())

        def end_graph(eng, go):
            eng.sem_inc(S["turn_over"], 1)
            eng.wait_ge(S[go], 1)
            eng.sem_clear(S[go])

        @block.sync
        def _(sp):
            with nc.allow_non_contiguous_dma("weights, once"):
                sp.dma_start(xin[:].rearrange("p (t d) -> p t d", d=D),
                             a["x"][0, :, :].rearrange("(t p) d -> p t d", p=P)).then_inc(S["x_in"], 16)
                sp.dma_start(prior[:].bitcast(I32), a["adj"].rearrange("(t p) n -> p t n", p=P)).then_inc(S["adj_in"], 16)
                for i, n in enumerate(SQUARE):
                    sp.dma_start(qz[:, 0, :][:, i * P:(i + 1) * P] if i < 8 else qz[:, 1, 0:P],
                                 a[n]).then_inc(S["weights_in"], 16)
                sp.dma_start(w1[:, 0:P], a["L1_gnn_W"]).then_inc(S["weights_in"], 16)
                sp.dma_start(w3[:, 0:P].rearrange("p (h f) -> p h f", h=H3),
                             a["L3_gnn_W"].rearrange("h d f -> d h f")).then_inc(S["weights_in"], 16)
                sp.dma_start(a1b, a["L1_gnn_a"].rearrange("(o n) c -> o (n c)", o=1).broadcast_to((P, 2 * P))).then_inc(S["weights_in"], 16)
                for i, n in enumerate(["L3_gnn_a_src", "L3_gnn_a_dst"]):
                    sp.dma_start(a3b[:, i, :], a[n].rearrange("(o h) f -> o (h f)", o=1).broadcast_to((P, P))).then_inc(S["weights_in"], 16)
                for i, n in enumerate(COLS):
                    sp.dma_start(cols[:, i:i + 1], a[n].rearrange("(p o) -> p o", o=1)).then_inc(S["weights_in"], 16)
                for i, n in enumerate(ROWS):
                    sp.dma_start(rows[:, i, :], a[n].rearrange("(o n) -> o n", o=1).broadcast_to((P, P))).then_inc(S["weights_in"], 16)
                sp.dma_start(beta3[:, 0:1], a["L3_gnn_beta_tilde"].broadcast_to((P, 1))).then_inc(S["weights_in"], 16)
            sp.sem_inc(S["x_stored"], 16)
            with sp.Fori(0, B) as b:
                sp.wait_ge(S["xin_used"], 1)
                nxt = (b + 1) % B
                sp.dma_start(xin[:].rearrange("p (t d) -> p t d", d=D),
                             a["x"][bass.ds(nxt, 1), :, :].rearrange("o (t p) d -> p (o t) d", p=P)).then_inc(S["x_in"], 16)
                sp.wait_ge(S["x_done"], 1)
                sp.dma_start(out[bass.ds(b, 1), :, :].rearrange("o (t p) d -> p (o t) d", p=P),
                             xs[:].rearrange("p (t d) -> p t d", d=D)).then_inc(S["x_stored"], 16)
                sp.wait_ge(S["turn_over"], 4)
                sp.sem_clear(range(numbers[0], numbers[-1] + 1))
                for name in ("go_pe", "go_act", "go_v", "go_pool"):
                    sp.sem_inc(S[name], 1)
            sp.wait_ge(S["x_stored"], 16)

        n_weights = 16 * (len(SQUARE) + 2 + 1 + 2 + len(COLS) + len(ROWS) + 1)

        @block.gpsimd
        def _(pool):
            pool.memset(ident[:], 0.0).then_inc(S["pool_link"], 1)
            pool.wait_ge(S["pool_link"], 1)
            pool.affine_select(out=ident[:], in_=ident[:], compare_op=ALU.not_equal, fill=1.0, base=0,
                               pattern=[[-1, P]], channel_multiplier=1).then_inc(S["pool_link"], 1)
            pool.wait_ge(S["pool_link"], 2)
            pool.memset(ones[:], 1.0)
            pool.memset(v3[:], 0.0).then_inc(S["consts"], 1)
            pool.wait_ge(S["wt_copied"], 1)
            pool.memset(qz[:], 0.0).then_inc(S["qz_zero"], 1)
            pool.wait_ge(S["af_ready"], 1)
            for t in range(T // 2, T):
                last = pool.tensor_scalar(maskN[:, t, :], ring[:, t, :], 0.0, -BIG, ALU.is_equal, ALU.mult)
            last.then_inc(S["af_used"], 1)
            for c in range(T):
                pool.wait_ge(S["adjT_read"], c + 1)
                pool.wait_ge(S["g_log"], c + 1)
                pool.tensor_tensor(prior[:, c, :], prior[:, c, :], mask1[:, c, :], ALU.mult)
            pool.wait_ge(S["first_hT_psum"], 1)
            with pool.Fori(0, B) as b:
                pool.tensor_scalar(hn[:], hn[:], 0.0, None, ALU.max).then_inc(S["pool_graph_link"], 1)
                pool.wait_ge(S["pool_graph_link"], 1)
                pool.tensor_tensor(blocks(hn[:]), blocks(hn[:]), repeat(rows[:, BO0, :], T), ALU.add)
                pool.tensor_tensor(blocks(xin[:]), blocks(xin[:]), repeat(rows[:, BETA, :], T),
                                   ALU.add).then_inc(S["biased"], 1)
                for m in range(CHUNKS0):
                    if m % T:
                        half = slice(m // T * HALF, (m // T + 1) * HALF)
                        pool.wait_ge(S["ctx0_read"], m + 1)
                        if m % T > 1:
                            pool.wait_ge(S["ctx0_added"], m - m // T - 1)
                        pool.tensor_tensor(ctx0[:, half], ctx0[:, half], part0[:, m % 2, :],
                                           ALU.add).then_inc(S["ctx0_added"], 1)
                pool.wait_ge(S["h_ready"], 4)
                pool.tensor_tensor(blocks(xs[:]), blocks(xs[:]), repeat(rows[:, BO2, :], T),
                                   ALU.add).then_inc(S["biased"], 1)
                for n in range(CHUNKS3):
                    for i in range(NH):
                        cs = slice(i * HALF, (i + 1) * HALF)
                        tile = ring3[(4 * n + 3) % RING3][:, cs]
                        pool.wait_ge(S["t3_ready"], NH * n + i + 1)
                        pool.tensor_tensor(tile, tile, prior[:, n % T, cs], ALU.mult).then_inc(S["p3_pool"], 1)
                end_graph(pool, "go_pool")

        @block.tensor
        def _(pe):
            mm = nc.tensor.matmul

            def transpose_blocks(dst, src):
                for t in range(T):
                    last = nc.tensor.transpose(dst[:, t * P:(t + 1) * P], src[:, t * P:(t + 1) * P], ident[:])
                return last

            pe.wait_ge(S["consts"], 1)
            pe.wait_ge(S["weights_in"], n_weights)
            last = transpose_blocks(slot[0], qz[:, 0, :])
            nc.tensor.transpose(slot[1][:, 0:P], qz[:, 1, 0:P], ident[:]).then_inc(S["wt_psum"], 1)
            def transpose_half(dst, src, i):
                for t in range(i * T // 2, (i + 1) * T // 2):
                    last = nc.tensor.transpose(dst[:, t * P:(t + 1) * P], src[:, t * P:(t + 1) * P], ident[:])
                return last

            def h_transposed(layer, src, i):
                pe.wait_ge(S["h_ready"], 2 * (layer - 1) + i + 1)
                transpose_half(slot[0], src, i).then_inc(S["hT_psum"], 1)

            def project_T(layer, dst, w, i):
                pe.wait_ge(S["hT_ready"], 2 * (layer - 1) + i + 1)
                return mm(dst[:, i * HALF:(i + 1) * HALF], w, hT[:, i * HALF:(i + 1) * HALF],
                          start=True, stop=True)

            def project_rows(dst, lhs, w, i):
                for t in range(i * T // 2, (i + 1) * T // 2):
                    last = mm(dst[:, t * P:(t + 1) * P], lhs[:, t * P:(t + 1) * P], w, start=True, stop=True)
                return last

            def queries_keys2():
                for i in range(2):
                    h_transposed(2, hx, i)
                    q = project_T(2, slot[1], wT[:, 4 + WQ, :], i)
                    last = project_T(2, slot[2], wT[:, 4 + WK, :], i)
                q.then_inc(S["q_psum"], 1)
                last.then_inc(S["k_psum"], 1)
                pe.wait_ge(S["kT_ready"], 1)

            def all_queries2():
                pe.wait_ge(S["qz_ready"], 3)
                pe.wait_ge(S["qz3_ready"], 1)

            def head_transpose(when):
                transpose_blocks(slot[2], hn).then_inc(S[when + "_hT_psum"], 1)

            def head_keys(when):
                pe.wait_ge(S[when + "_hT"], 1)
                for i in range(2):
                    cs = slice(i * HALF, (i + 1) * HALF)
                    last = mm(slot[2][:, cs], wT[:, WK, :], hT0[:, cs], start=True, stop=True)
                last.then_inc(S[when + "_k_psum"], 1)

            def head_queries(when):
                pe.wait_ge(S[when + "_kT"], 1)
                for i in range(2):
                    cs = slice(i * HALF, (i + 1) * HALF)
                    last = mm(slot[2][:, cs], wT[:, WQ, :], hT0[:, cs], start=True, stop=True)
                last.then_inc(S[when + "_q_psum"], 1)

            def project_values(k, src):
                for i in range(2):
                    last = project_rows(acc[:].rearrange("p i c -> p (i c)"), src, wT[:, 4 * k + WV, :], i)
                last.then_inc(S["v_psum"], 1)

            def layer0(b):
                def scores(u):
                    n, pair = u // 2, u % 2
                    half, c = n // T, n % T
                    if u == O0_AT + 2:
                        pe.wait_ge(S["o0_read"], 1)
                    elif u >= 3:
                        pe.wait_ge(S["e0_done"], u - 2 if u < O0_AT or u >= O0_AT + 3 else u - 1)
                    for i in range(2):
                        last = mm(slot[slot0(u)][:, i * HALF:(i + 1) * HALF], kT[:, c * P:(c + 1) * P],
                                  qz[:, 2 * pair + i, half * HALF:(half + 1) * HALF], start=True, stop=True)
                    last.then_inc(S["s0_ready"], 1)

                def values(m):
                    c = m % T
                    pe.wait_ge(S["p0_ready"], 2 * m + 2)
                    if m == 0:
                        pe.wait_ge(S["v_ready"], 1)
                    if m >= 1:
                        pe.wait_ge(S["ctx0_read"], m)
                        pe.wait_ge(S["z0_read"], m)
                    for k in range(2):
                        for h in range(H0):
                            lhs = vn[:, c * P + h * DH0:c * P + (h + 1) * DH0] if k == 0 else ones[:, 0:DH0]
                            last = mm(acc[h * DH0:(h + 1) * DH0, k, :], lhs,
                                      ring[:, (2 * m + h // 2) % RING, (h % 2) * HALF:(h % 2 + 1) * HALF],
                                      start=True, stop=True)
                    last.then_inc(S["pv0_done"], 1)

                for n in range(CHUNKS0):
                    scores(2 * n)
                    scores(2 * n + 1)
                    if n == 0:
                        project_values(0, hT0)
                    if 2 * n + 2 == O0_AT:
                        pe.wait_ge(S["ctx0_added"], T - 1)
                        pe.wait_ge(S["ctx0_read"], T)
                        pe.wait_ge(S["e0_done"], O0_AT - 2)
                        project_rows(slot[O0_AT % 3], ctx0, wT[:, WO, :], 0).then_inc(S["o0_psum"], 1)
                    if n:
                        values(n - 1)
                values(CHUNKS0 - 1)
                pe.wait_ge(S["ctx0_read"], CHUNKS0)
                pe.wait_ge(S["ctx0_added"], CHUNKS0 - NH)
                project_rows(slot[0], ctx0, wT[:, WO, :], 1).then_inc(S["o0_psum"], 1)

            def layer1(b):
                for i in range(2):
                    last = project_T(1, slot[1], wa1[:, 1:2].broadcast_to((P, P)), i)
                last.then_inc(S["d1_psum"], 1)
                for i in range(2):
                    last = project_T(1, slot[2], wa1[:, 0:1].broadcast_to((P, P)), i)
                last.then_inc(S["s1_psum"], 1)
                for t in range(T):
                    if t == T // 2:
                        pe.wait_ge(S["dmax1_ready"], 1)
                    last = mm(psum[:, t // 4, t % 4 * 256:t % 4 * 256 + P + 1], hT[:, t * P:(t + 1) * P], w1[:],
                              start=True, stop=True)
                last.then_inc(S["v1_psum"], 1)
                for i in range(2):
                    for c in range(T):
                        if i == 0:
                            pe.wait_ge(S["p1_ready"], c + 1)
                        for t in range(T // 2):
                            q = (i * T // 2 + t) * P
                            last = mm(sums1[i][:, t, 0:P + 1], tiles1[c][:, q:q + P], v1[:, c, 0:P + 1],
                                      start=(c == 0 and t % 2 == 0), stop=(c == T - 1 and t % 2 == 1))
                    last.then_inc(S["n1_psum"], 1)

            def s_slot(w):
                return 0 if w == 0 else (2 * w - 1) % 3

            def t_slot(w):
                return (2 * w + 2) % 3

            def layer2(b):
                def scores(w):
                    blk, h = w // H0, w % H0
                    if w == 0:
                        pe.wait_ge(S["qz_ready"], 1)
                    if w == 1:
                        all_queries2()
                    if w == 2:
                        pe.wait_ge(S["p2_ready"], 1)
                    if w >= 3:
                        pe.wait_ge(S["t2_even"], w - 2)
                        pe.wait_ge(S["t2_odd"], w - 2)
                    for i in range(NH):
                        cs = slice(i * HALF, (i + 1) * HALF)
                        last = mm(slot[s_slot(w)][:, cs], qz[:, h, blk * P:(blk + 1) * P], kT[:, cs],
                                  start=True, stop=True)
                    last.then_inc(S["s2_ready"], 1)

                def transposed(w):
                    pe.wait_ge(S["p2_ready"], w + 1)
                    transpose_blocks(slot[t_slot(w)], ring[:, w % RING, :]).then_inc(S["t2_psum"], 1)

                def values(blk):
                    pe.wait_ge(S["t2_even"], H0 * (blk + 1))
                    pe.wait_ge(S["t2_odd"], H0 * (blk + 1))
                    for c in range(T):
                        for h in range(H0):
                            last = mm(acc[h * DH0:(h + 1) * DH0, blk // 4, blk % 4 * P:(blk % 4 + 1) * P],
                                      vn[:, c * P + h * DH0:c * P + (h + 1) * DH0], pT[:, h, c * P:(c + 1) * P],
                                      start=(c == 0), stop=(c == T - 1))
                    last.then_inc(S["pv2_done"], 1)

                scores(0)
                for w in range(UNITS2):
                    if w + 1 < UNITS2:
                        scores(w + 1)
                    if w == 0:
                        project_values(1, hT)
                    if w == H0:
                        pe.wait_ge(S["v_ready"], 2)
                    if w and w % H0 == 0:
                        values(w // H0 - 1)
                    transposed(w)
                values(T - 1)
                for i in range(2):
                    pe.wait_ge(S["c2_ready"], i + 1)
                    transpose_half(slot[0], tA, i).then_inc(S["cn2_psum"], 1)
                for i in range(2):
                    pe.wait_ge(S["cn2_ready"], i + 1)
                    transpose_half(slot[1], tB, i).then_inc(S["cT2_psum"], 1)
                for i in range(2):
                    pe.wait_ge(S["cT2_ready"], i + 1)
                    project_rows(slot[2], tC, wT[:, 4 + WO, :], i).then_inc(S["o2_psum"], 1)

            def layer3(b):
                for s, name in ((1, "d3_psum"), (2, "s3_psum")):
                    for i in range(NH):
                        cs = slice(i * HALF, (i + 1) * HALF)
                        pe.wait_ge(S["hT_ready"], 4 + i + 1)
                        last = mm(psum[:, s, cs], w3w[:, s - 1, :], hT[:, cs], start=True, stop=True)
                    last.then_inc(S[name], 1)
                for i in range(NH):
                    mm(acc[:, 1, 0:P], hsum[:, i:i + 1].broadcast_to((P, P)), w3[:, 0:P], start=(i == 0), stop=(i == 1))
                pe.wait_ge(S["dmax3_ready"], 1)
                mm(acc[:, 0, 0:H3], ones[:], diag3[:], start=True, stop=True).then_inc(S["dmaxb3_psum"], 1)
                for t in range(T):
                    last = mm(psum[:, t // 4, t % 4 * 256:t % 4 * 256 + P + H3], hT[:, t * P:(t + 1) * P], w3[:],
                              start=True, stop=True)
                last.then_inc(S["v3_psum"], 1)

                def row_factors(h, dst):
                    for i in range(NH):
                        cs = slice(i * HALF, (i + 1) * HALF)
                        last = mm(dst[i], ident[:, h * DH3:h * DH3 + 1].broadcast_to((P, P)), tB[:, cs],
                                  start=True, stop=True)
                    last.then_inc(S["r3_psum"], 1)

                accs = [acc[:, i, :] for i in range(NH)]
                slots = [[slot[k][:, i * HALF:(i + 1) * HALF] for i in range(NH)] for k in range(3)]
                pe.wait_ge(S["r3_ready"], 1)
                pe.wait_ge(S["sums3_read"], 1)
                row_factors(3, accs)
                pe.wait_ge(S["v3_ready"], 1)
                for h in range(3):
                    row_factors(h, slots[h])
                pe.wait_ge(S["fac3_ready"], 1)
                row_factors(7, accs)
                pe.wait_ge(S["fac3_ready"], 2)
                for n in range(CHUNKS3):
                    g, c = n // T, n % T
                    if n == T - 1:
                        for k in range(3):
                            pe.wait_ge(S["p3_ready"], 3 * n + k + 1)
                            row_factors(4 + k, slots[k])
                    pe.wait_ge(S["p3_ready"], 3 * n + 3)
                    if n == T:
                        pe.wait_ge(S["o3_ready"], 1)
                    for i in range(NH):
                        pe.wait_ge(S["p3_pool"], NH * n + i + 1)
                        for h in range(4):
                            last = mm(acc[32 * h:32 * h + 32, i, :], v3[:, c, 4 * g + h, :],
                                      ring3[(4 * n + h) % RING3][:, i * HALF:(i + 1) * HALF],
                                      start=(c == 0), stop=(c == T - 1))
                        if n == CHUNKS3 - 1 and i == 0:
                            last.then_inc(S["pv3_done"], 1)
                    last.then_inc(S["pv3_done"], 1)
                    if n == T:
                        pe.wait_ge(S["fac3_ready"], 3)
                        transpose_blocks(slot[2], tA).then_inc(S["on3_psum"], 1)
                    if n == T + 3:
                        pe.wait_ge(S["slot2_read"], 1)
                        head_transpose("next")
                    if n == T + 4:
                        head_keys("next")
                    if n == T + 5:
                        head_queries("next")
                for i in range(2):
                    pe.wait_ge(S["o3_ready"], i + 2)
                    transpose_half(slot[1], tC, i).then_inc(S["on3_psum"], 1)
                for i in range(2):
                    pe.wait_ge(S["next_q"], 1)
                    pe.wait_ge(S["cn3_ready"], i + 1)
                    transpose_half(slot[2], cn3, i).then_inc(S["cT3_psum"], 1)
                for i in range(2):
                    pe.wait_ge(S["cT3_ready"], i + 1)
                    project_rows(slot[0], tA, wT[:, WOUT3, :], i).then_inc(S["o3_psum"], 1)

            pe.wait_ge(S["h_first"], 1)
            head_transpose("first")
            head_keys("first")
            head_queries("first")
            pe.wait_ge(S["amax_t"], 1)
            nc.tensor.transpose(acc[0:1, 0, 0:P], amax[:, 0:1], ident[:]).then_inc(S["amax_tr"], 1)
            pe.wait_ge(S["amax_row"], 1)
            mm(acc[:, 1, 0:1], ones[0:1, :], amax[0:1, 1:2], start=True, stop=True).then_inc(S["amax_b"], 1)
            pe.wait_ge(S["first_q"], 1)
            for c in range(T):
                if c >= 3:
                    pe.wait_ge(S["adjT_taken"], c - 2)
                for t in range(T):
                    last = nc.tensor.transpose(slot[c % 3][:, t * P:(t + 1) * P],
                                               ring[:, t, c * P:(c + 1) * P], ident[:])
                last.then_inc(S["adjT_psum"], 1)
            pe.wait_ge(S["adjT_taken"], T)
            pe.wait_ge(S["wa_ready"], 1)
            with pe.Fori(0, B) as b:
                layer0(b)
                for i in range(2):
                    h_transposed(1, hx, i)
                layer1(b)
                queries_keys2()
                layer2(b)
                for i in range(2):
                    h_transposed(3, hx, i)
                layer3(b)
                end_graph(pe, "go_pe")

        @block.scalar
        def _(act):
            link = Links(act, S["act_setup_link"])
            go = nc.scalar.activation
            act.add_instruction(mybir.InstLoadActFuncSet(act_func_set_id=EXP_AND_LN, name=nc.get_next_instruction_name(),
                                                         engine=mybir.EngineType.Activation))

            isds = [0]

            def inverse_deviation(halves, first=False):
                ts = slice(0, T) if halves is None else slice(halves * T // 2, (halves + 1) * T // 2)
                if not first:
                    isds[0] += 1
                act.wait_ge(S["var_first" if first else "var_ready"], 1 if first else isds[0])
                link(go(lnv[:, ts], veps[:, ts], ACT.Ln))
                go(isd[:, ts], lnv[:, ts], ACT.Exp, scale=-0.5).then_inc(S["isd_first" if first else "isd_ready"], 1)

            def h_transposed(layer, halves=range(2)):
                for i in halves:
                    act.wait_ge(S["hT_psum"], 2 * (layer - 1) + i + 1)
                    cs = slice(i * HALF, (i + 1) * HALF)
                    go(hT[:, cs], slot[0][:, cs], ACT.Relu, accum_out=hsum[:, i:i + 1]).then_inc(S["hT_ready"], 1)

            def spread_q2():
                act.wait_ge(S["q_psum"], 1)
                for h in range(H0 - 1):
                    ps = slice(h * DH0, (h + 1) * DH0)
                    go(qz[ps, h, :], psum[ps, 1, :], ACT.Identity, bias=cols[ps, 2:3]).then_inc(S["qz_ready"], 1)

            def head_transposed(when):
                act.wait_ge(S[when + "_hT_psum"], 1)
                go(hT0, slot[2], ACT.Relu).then_inc(S[when + "_hT"], 1)

            def head_keys(when):
                act.wait_ge(S[when + "_k_psum"], 1)
                go(kT[:], slot[2], ACT.Identity, bias=cols[:, 1:2]).then_inc(S[when + "_kT"], 1)

            def head_queries(when):
                act.wait_ge(S[when + "_q_psum"], 1)
                for h in range(H0):
                    ps = slice(h * DH0, (h + 1) * DH0)
                    last = go(qz[ps, h, :], psum[ps, 2, :], ACT.Identity, bias=cols[ps, 0:1])
                last.then_inc(S[when + "_q"], 1)

            def layer0(b):
                def weights(u):
                    act.wait_ge(S["s0_ready"], u + 1)
                    if u >= RING:
                        act.wait_ge(S["pv0_done"], (u - RING) // 2 + 1)
                    go(ring[:, u % RING, :], slot[slot0(u)], ACT.Exp, scale=SCALE).then_inc(S["e0_done"], 1)

                def inverse_sums(m):
                    act.wait_ge(S["pv0_done"], m + 1)
                    if m >= 2:
                        act.wait_ge(S["ctx0_read"], m - 1)
                    go(rzs[:, m % 2, :], acc[:, 1, :], ACT.Ln).then_inc(S["z0_read"], 1)
                    act.wait_ge(S["z0_read"], m + 1)
                    go(rzs[:, m % 2, :], rzs[:, m % 2, :], ACT.Exp, scale=-1.0).then_inc(S["rz0_ready"], 1)

                for n in range(CHUNKS0):
                    if n >= 2:
                        inverse_sums(n - 2)
                    weights(2 * n)
                    if n in (O0_AT // 2 + 1, O0_AT // 2 + 2):
                        inverse_deviation(0)
                    weights(2 * n + 1)
                inverse_sums(CHUNKS0 - 2)
                inverse_sums(CHUNKS0 - 1)

            def layer1(b):
                act.wait_ge(S["s1_shifted"], 1)
                go(tB[:], tA[:], ACT.Exp, scale=-(1 - ALPHA)).then_inc(S["r1_ready"], 1)
                act.wait_ge(S["dm1_ready"], 1)
                go(c1, dm1, ACT.Exp, scale=1 - ALPHA)
                go(d1, dm1, ACT.Exp, scale=ALPHA).then_inc(S["c1_ready"], 1)
                for i in range(2):
                    cs = slice(i * HALF, (i + 1) * HALF)
                    act.wait_ge(S["neg1_ready"], i + 1)
                    go(tC[:, cs], tC[:, cs], ACT.Exp).then_inc(S["e1_ready"], 1)
                    inverse_deviation(i)
                    h_transposed(2, [i])

            def layer2(b):
                def weights(w):
                    act.wait_ge(S["nm2_ready"], w + 1)
                    if w >= RING:
                        act.wait_ge(S["t2_psum"], w - RING + 1)
                    go(ring[:, w % RING, :], slot[0 if w == 0 else (2 * w - 1) % 3], ACT.Exp, scale=-1.0,
                       bias=nm2[:, w:w + 1], accum_out=z2[:, w:w + 1]).then_inc(S["p2_ready"], 1)

                def copy_odd(w):
                    act.wait_ge(S["t2_psum"], w + 1)
                    if w >= H0:
                        act.wait_ge(S["pv2_done"], w // H0)
                    go(pT[:, w % H0, HALF:N], psum[:, (2 * w + 2) % 3, HALF:N], ACT.Copy).then_inc(S["t2_odd"], 1)

                def context(i):
                    act.wait_ge(S["pv2_done"], (i + 1) * T // 2)
                    go(tA[:, i * HALF:(i + 1) * HALF], acc[:, i, :], ACT.Copy).then_inc(S["c2_ready"], 1)

                for w in range(UNITS2):
                    weights(w)
                    if w:
                        copy_odd(w - 1)
                    if w == NEXT_NORM_AT + 2:
                        inverse_deviation(None)
                    if w == UNITS2 // 2 + 4:
                        context(0)
                copy_odd(UNITS2 - 1)
                context(1)
                for i in range(2):
                    cs = slice(i * HALF, (i + 1) * HALF)
                    act.wait_ge(S["cn2_ready"], 2)
                    act.wait_ge(S["cT2_psum"], i + 1)
                    go(tC[:, cs], slot[1][:, cs], ACT.Copy).then_inc(S["cT2_ready"], 1)

            def layer3(b):
                act.wait_ge(S["s3_shifted"], 1)
                go(tB[:], tA[:], ACT.Exp, scale=-(1 - ALPHA)).then_inc(S["r3_ready"], 1)
                act.wait_ge(S["dm3_ready"], 1)
                go(c3, dm3, ACT.Exp, scale=1 - ALPHA)
                go(d3, dm3, ACT.Exp, scale=ALPHA).then_inc(S["c3_ready"], 1)

                def keep_factors(h, order, src):
                    act.wait_ge(S["r3_psum"], order)
                    go(fac3[h], src, ACT.Copy).then_inc(S["fac3_ready"], 1)

                accs = acc[:].rearrange("p i c -> p (i c)")
                act.wait_ge(S["nc3_ready"], 1)
                keep_factors(3, 1, accs)
                for n in range(CHUNKS3):
                    h, c = 4 * (n // T) + 3, n % T
                    if n >= 2:
                        act.wait_ge(S["pv3_done"], n - 1)
                    if n % T == 0:
                        act.wait_ge(S["fac3_ready"], 1 + n // T)
                    for i in range(NH):
                        cs = slice(i * HALF, (i + 1) * HALF)
                        tile = ring3[(4 * n + 3) % RING3][:, cs]
                        link(go(tile, fac3[h][:, cs], ACT.Relu, bias=nc3[:, c, h:h + 1]))
                        go(tile, tile, ACT.Identity, bias=c3[:, c, h:h + 1]).then_inc(S["t3_ready"], 1)
                    if n == 0:
                        keep_factors(7, 5, accs)
                    if n == T:
                        act.wait_ge(S["p3_ready"], 3 * T + 3)
                        keep_factors(6, 8, slot[2])
                        act.wait_ge(S["pv3_done"], T)
                        go(tA[:], accs, ACT.Copy).then_inc(S["o3_ready"], 1)
                    if n == T + 5:
                        head_transposed("next")
                    if n == T + 6:
                        head_keys("next")
                    if n == T + 7:
                        head_queries("next")
                for i in range(2):
                    act.wait_ge(S["pv3_done"], CHUNKS3 + i)
                    go(tC[:, i * HALF:(i + 1) * HALF], acc[:, i, :], ACT.Copy).then_inc(S["o3_ready"], 1)
                for i in range(2):
                    cs = slice(i * HALF, (i + 1) * HALF)
                    act.wait_ge(S["cT3_psum"], i + 1)
                    go(tA[:, cs], slot[2][:, cs], ACT.Copy).then_inc(S["cT3_ready"], 1)

            inverse_deviation(None, first=True)
            act.wait_ge(S["wt_psum"], 1)
            go(wT[:, 0:8, :].rearrange("p w o -> p (w o)"), slot[0], ACT.Copy)
            go(wT[:, 8, :], slot[1][:, 0:P], ACT.Copy).then_inc(S["wt_copied"], 1)
            head_transposed("first")
            act.wait_ge(S["weights_in"], n_weights)
            head_keys("first")
            act.wait_ge(S["qz_zero"], 1)
            head_queries("first")
            act.wait_ge(S["beta_e"], 1)
            link(go(beta3[:, 1:2], beta3[:, 1:2], ACT.Exp, scale=-1.0))
            go(beta3[:, 1:2], beta3[:, 1:2], ACT.Ln, bias=1.0).then_inc(S["beta_ready"], 1)
            act.wait_ge(S["beta_e"], 2)
            act.wait_ge(S["adjf"], 2)
            for c in range(T):
                act.wait_ge(S["adjT_read"], c + 1)
                go(prior[:, c, :], slot[c % 3], ACT.Relu).then_inc(S["adjT_taken"], 1)
                act.wait_ge(S["adjT_taken"], c + 1)
                link(go(prior[:, c, :], prior[:, c, :], ACT.Ln, scale=amax[:, 3:4], bias=amax[:, 4:5]))
                go(prior[:, c, :], prior[:, c, :], ACT.Exp, scale=beta3[:, 2:3]).then_inc(S["g_log"], 1)
            act.wait_ge(S["af_used"], 1)
            link = Links(act, S["act_link"])
            with act.Fori(0, B) as b:
                layer0(b)
                inverse_deviation(1)
                inverse_deviation(1)
                h_transposed(1)
                layer1(b)
                spread_q2()
                layer2(b)
                inverse_deviation(0)
                inverse_deviation(1)
                h_transposed(3)
                layer3(b)
                end_graph(act, "go_act")

        @block.vector
        def _(v):
            link = Links(v, S["dve_setup_link"])

            isds = [0]

            def half_blocks(i):
                return range(T) if i is None else range(i * T // 2, (i + 1) * T // 2)

            def norm_stats(i, src, first=False):
                ts = half_blocks(i)
                for t in ts:
                    last = v.bn_stats(bnst[:, t, :], src[:, t * P:(t + 1) * P])
                link(last)
                for t in ts:
                    last = v.bn_aggr(mv[:, t, :], bnst[:, t, :])
                link(last)
                cs = slice(ts[0], ts[-1] + 1)
                v.tensor_scalar(veps[:, cs], mv[:, cs, 1], LN_EPS, None,
                                ALU.add).then_inc(S["var_first" if first else "var_ready"], 1)

            def norm_apply(i, dst, src, first=False):
                ts = half_blocks(i)
                cs = slice(ts[0], ts[-1] + 1)
                if not first:
                    isds[0] += 1
                v.wait_ge(S["isd_first" if first else "isd_ready"], 1 if first else isds[0])
                link(v.tensor_tensor(nwt[:, cs], isd[:, cs], isd[:, cs], ALU.mult))
                link(v.scalar_tensor_tensor(out=nwt[:, cs], in0=nwt[:, cs], scalar=-0.5, in1=veps[:, cs],
                                            op0=ALU.mult, op1=ALU.mult))
                link(v.scalar_tensor_tensor(out=rstd[:, cs], in0=nwt[:, cs], scalar=1.5, in1=isd[:, cs],
                                            op0=ALU.add, op1=ALU.mult))
                for t in ts:
                    bs = slice(t * P, (t + 1) * P)
                    last = v.tensor_scalar(dst[:, bs], src[:, bs], mv[:, t, 0:1], rstd[:, t:t + 1],
                                           ALU.subtract, ALU.mult)
                return last

            def pre_norm_apply():
                for i in range(2):
                    norm_apply(i, hx, xs).then_inc(S["h_ready"], 1)

            def queries_keys2():
                v.wait_ge(S["k_psum"], 1)
                v.tensor_scalar(kT[:], slot[2], cols[:, 3:4], None, ALU.add).then_inc(S["kT_ready"], 1)
                ps = slice((H0 - 1) * DH0, P)
                v.wait_ge(S["q_psum"], 1)
                v.tensor_scalar(qz[ps, H0 - 1, :], psum[ps, 1, :], cols[ps, 2:3], None,
                                ALU.add).then_inc(S["qz3_ready"], 1)

            def values(k):
                v.wait_ge(S["v_psum"], k + 1)
                v.tensor_tensor(blocks(vn[:]), blocks(acc[:].rearrange("p i c -> p (i c)")),
                                repeat(rows[:, (BV0, BV2)[k], :], T), ALU.add).then_inc(S["v_ready"], 1)

            def layer0(b):
                adds = CHUNKS0 - NH
                v.wait_ge(S["x_stored"], 16)
                v.sem_clear(S["x_stored"])

                def clip(u):
                    n = u // 2
                    half, c = n // T, n % T
                    v.wait_ge(S["e0_done"], u + 1)
                    tile = ring[:, u % RING, :].rearrange("p (i c) -> p i c", i=2)
                    v.scalar_tensor_tensor(out=tile, in0=tile, scalar=E_LO,
                                           in1=repeat(clipU[:, c, half * HALF:(half + 1) * HALF], 2),
                                           op0=ALU.max, op1=ALU.min).then_inc(S["p0_ready"], 1)

                def scale(m):
                    v.wait_ge(S["rz0_ready"], m + 1)
                    half = slice(m // T * HALF, (m // T + 1) * HALF)
                    if m % T and m >= 2 and (m - 2) % T:
                        v.wait_ge(S["ctx0_added"], (m - 2) - (m - 2) // T)
                    dst = part0[:, m % 2, :] if m % T else ctx0[:, half]
                    v.tensor_tensor(dst, acc[:, 0, :], rzs[:, m % 2, :], ALU.mult).then_inc(S["ctx0_read"], 1)

                def residual(i):
                    cs = slice(i * HALF, (i + 1) * HALF)
                    v.wait_ge(S["biased"], 1)
                    v.wait_ge(S["o0_psum"], i + 1)
                    link(v.tensor_tensor(tA[:, cs], slot[O0_AT % 3 if i == 0 else 0][:, cs], hn[:, cs], ALU.add))
                    v.sem_inc(S["o0_read"], 1)
                    norm_stats(i, tA)

                def finish(i):
                    cs = slice(i * HALF, (i + 1) * HALF)
                    link(norm_apply(i, tA, tA))
                    link(v.tensor_tensor(blocks(tA[:, cs]), blocks(tA[:, cs]), repeat(rows[:, GAMMA, :], T // 2),
                                         ALU.mult))
                    link(v.tensor_tensor(xs[:, cs], xin[:, cs], tA[:, cs], ALU.add))
                    norm_stats(i, xs)

                for n in range(CHUNKS0):
                    if n >= 2:
                        scale(n - 2)
                    clip(2 * n)
                    clip(2 * n + 1)
                    if n == 0:
                        values(0)
                    if n == O0_AT // 2:
                        residual(0)
                    if n == O0_AT // 2 + 1:
                        finish(0)
                    if n == O0_AT // 2 + 2:
                        norm_apply(0, hx, xs).then_inc(S["h_ready"], 1)
                scale(CHUNKS0 - 2)
                scale(CHUNKS0 - 1)
                residual(1)
                finish(1)
                v.sem_inc(S["xin_used"], 1)
                norm_apply(1, hx, xs).then_inc(S["h_ready"], 1)

            def layer1(b):
                v.wait_ge(S["d1_psum"], 1)
                link(v.tensor_reduce(dmax1[:], slot[1], AX.X, ALU.max))
                v.sem_inc(S["dmax1_ready"], 1)
                v.wait_ge(S["s1_psum"], 1)
                v.tensor_scalar(tA[:], slot[2], dmax1[:, 0:1], -100.0, ALU.add, ALU.max).then_inc(S["s1_shifted"], 1)
                v.wait_ge(S["v1_psum"], 1)
                view = psum[:, 0:2, :].rearrange("p s (k c) -> p (s k) c", c=256)
                v.tensor_scalar(dm1, view[:, :, P], dmax1[:, 0:1], None, ALU.subtract).then_inc(S["dm1_ready"], 1)
                v.wait_ge(S["c1_ready"], 1)
                v.tensor_copy(v1[:, :, P], d1)
                v.tensor_tensor(v1[:, :, 0:P], view[:, :, 0:P], spread(d1, P), ALU.mult)
                v.wait_ge(S["r1_ready"], 1)
                for c in range(T):
                    v.scalar_tensor_tensor(out=tiles1[c], in0=tB[:], scalar=c1[:, c:c + 1],
                                           in1=mask1[:, c, :], op0=ALU.max, op1=ALU.mult).then_inc(S["p1_ready"], 1)
                for i in range(2):
                    cs, ts = slice(i * HALF, (i + 1) * HALF), slice(i * T // 2, (i + 1) * T // 2)
                    v.wait_ge(S["n1_psum"], i + 1)
                    link(v.reciprocal(rz1[:, ts], sums1[i][:, :, P]))
                    link(v.tensor_tensor(blocks(tA[:, cs]), sums1[i][:, :, 0:P], spread(rz1[:, ts], P), ALU.mult))
                    v.tensor_scalar(tC[:, cs], tA[:, cs], 0.0, None, ALU.min).then_inc(S["neg1_ready"], 1)
                    link(v.scalar_tensor_tensor(out=tA[:, cs], in0=tA[:, cs], scalar=0.0, in1=xs[:, cs],
                                                op0=ALU.max, op1=ALU.add))
                    v.wait_ge(S["e1_ready"], i + 1)
                    link(v.scalar_tensor_tensor(out=xs[:, cs], in0=tC[:, cs], scalar=-1.0, in1=tA[:, cs],
                                                op0=ALU.add, op1=ALU.add))
                    norm_stats(i, xs)
                    norm_apply(i, hx, xs).then_inc(S["h_ready"], 1)

            def layer2(b):
                def row_max(w):
                    v.wait_ge(S["s2_ready"], w + 1)
                    tile = slot[0 if w == 0 else (2 * w - 1) % 3]
                    v.tensor_tensor_reduce(out=tile, in0=tile, in1=maskN[:, w // H0, :], scale=-SCALE, scalar=-FLOOR,
                                           op0=ALU.add, op1=ALU.min,
                                           accum_out=nm2[:, w:w + 1]).then_inc(S["nm2_ready"], 1)

                def copy_even(w):
                    v.wait_ge(S["t2_psum"], w + 1)
                    if w >= H0:
                        v.wait_ge(S["pv2_done"], w // H0)
                    v.tensor_copy(pT[:, w % H0, 0:HALF], psum[:, (2 * w + 2) % 3, 0:HALF]).then_inc(S["t2_even"], 1)

                for w in range(UNITS2):
                    row_max(w)
                    if w == 1:
                        values(1)
                    if w:
                        copy_even(w - 1)
                    if w == NEXT_NORM_AT:
                        v.wait_ge(S["x_in"], 16)
                        v.sem_clear(S["x_in"])
                        norm_stats(None, xin)
                    if w == NEXT_NORM_AT + 4:
                        norm_apply(None, hn, xin)
                copy_even(UNITS2 - 1)
                v.wait_ge(S["p2_ready"], UNITS2)
                link(v.tensor_scalar(z2, z2, 1e-30, None, ALU.max))
                link(v.reciprocal(rz2, z2))
                for i in range(2):
                    cs, ws = slice(i * HALF, (i + 1) * HALF), slice(i * UNITS2 // 2, (i + 1) * UNITS2 // 2)
                    v.wait_ge(S["cn2_psum"], i + 1)
                    v.tensor_tensor(tB[:, cs].rearrange("p (w d) -> p w d", d=DH0),
                                    slot[0][:, cs].rearrange("p (w d) -> p w d", d=DH0), spread(rz2[:, ws], DH0),
                                    ALU.mult).then_inc(S["cn2_ready"], 1)
                v.wait_ge(S["biased"], 2)
                for i in range(2):
                    cs = slice(i * HALF, (i + 1) * HALF)
                    v.wait_ge(S["o2_psum"], i + 1)
                    link(v.tensor_tensor(xs[:, cs], xs[:, cs], slot[2][:, cs], ALU.add))
                    norm_stats(i, xs)
                pre_norm_apply()

            def layer3(b):
                v.wait_ge(S["d3_psum"], 1)
                link(v.tensor_reduce(dmax3[:], slot[1], AX.X, ALU.max))
                v.tensor_scalar(diag3[:], ident[:].rearrange("p (h f) -> p h f", f=DH3)[:, :, 0], dmax3[:, 0:1], None,
                                ALU.mult).then_inc(S["dmax3_ready"], 1)
                v.wait_ge(S["s3_psum"], 1)
                v.tensor_scalar(tA[:], slot[2], dmax3[:, 0:1], -100.0, ALU.add,
                                ALU.max).then_inc(S["s3_shifted"], 1)
                v.wait_ge(S["v3_psum"], 1)
                view = psum[:, 0:2, :].rearrange("p s (k c) -> p (s k) c", c=256)
                v.wait_ge(S["dmaxb3_psum"], 1)
                link(v.tensor_copy(dmaxb3[:], acc[:, 0, 0:H3]))
                v.tensor_tensor(dm3, view[:, :, P:P + H3], repeat(dmaxb3[:], T), ALU.subtract).then_inc(S["dm3_ready"], 1)
                sums = sv3.rearrange("p (h f) -> p h f", h=H3)
                v.tensor_scalar(sums[:, :, DH3], ones[:, 0:H3], float(N), None, ALU.mult)
                v.tensor_copy(sums[:, :, 0:DH3], acc[:, 1, 0:P].rearrange("p (h f) -> p h f", h=H3)).then_inc(S["sums3_read"], 1)
                v.wait_ge(S["c3_ready"], 1)
                v.tensor_scalar(nc3, c3, -1.0, None, ALU.mult).then_inc(S["nc3_ready"], 1)
                v.tensor_copy(v3[:, :, :, DH3], d3)
                d3w = spread(d3.rearrange("p t h -> p (t h)"), DH3).rearrange("p (t h) f -> p t h f", h=H3)
                v.tensor_tensor(v3[:, :, :, 0:DH3], view[:, :, 0:P].rearrange("p t (h f) -> p t h f", h=H3), d3w,
                                ALU.mult).then_inc(S["v3_ready"], 1)

                def normalise(g, i):
                    ts = half_blocks(i)
                    for t in ts:
                        last = v.scalar_tensor_tensor(out=tB[:, t * P:(t + 1) * P], in0=sv3[:, g * P:(g + 1) * P],
                                                      scalar=empty3[:, t:t + 1], in1=slot[2 - g][:, t * P:(t + 1) * P],
                                                      op0=ALU.mult, op1=ALU.add)
                    link(last)
                    nat = tB[:].rearrange("p (w c) -> p w c", c=SLOT3)
                    ws = slice(4 * ts[0], 4 * ts[-1] + 4)
                    link(v.reciprocal(rz3[:, g, ws], nat[:, ws, DH3]))
                    for t in ts:
                        last = v.tensor_tensor(
                            cn3[:, t * P + g * 64:t * P + g * 64 + 64].rearrange("p (h f) -> p h f", h=4),
                            nat[:, 4 * t:4 * t + 4, 0:DH3], spread(rz3[:, g, 4 * t:4 * t + 4], DH3), ALU.mult)
                    return last

                for n in range(CHUNKS3):
                    g, c = n // T, n % T
                    for k in range(3):
                        h = 4 * g + k
                        if c == 0:
                            v.wait_ge(S["r3_psum"], (2 if g == 0 else 6) + k)
                        if n >= 2 and k == 0:
                            v.wait_ge(S["pv3_done"], n - 1)
                        if h == 6 and c == 1:
                            v.wait_ge(S["fac3_ready"], 3)
                        fac = fac3[6] if h == 6 and c else slot[k]
                        v.scalar_tensor_tensor(out=ring3[(4 * n + k) % RING3], in0=fac, scalar=c3[:, c, h:h + 1],
                                               in1=prior[:, c, :], op0=ALU.max, op1=ALU.mult).then_inc(S["p3_ready"], 1)
                    if n == T + 2:
                        v.wait_ge(S["on3_psum"], 1)
                        link(normalise(0, None))
                        v.sem_inc(S["slot2_read"], 1)
                for i in range(2):
                    v.wait_ge(S["on3_psum"], i + 2)
                    normalise(1, i).then_inc(S["cn3_ready"], 1)
                for i in range(2):
                    cs = slice(i * HALF, (i + 1) * HALF)
                    v.wait_ge(S["o3_psum"], i + 1)
                    last = v.tensor_tensor(xs[:, cs], xs[:, cs], slot[0][:, cs], ALU.add)
                link(last)
                v.sem_inc(S["x_done"], 1)

            v.wait_ge(S["x_in"], 16)
            v.sem_clear(S["x_in"])
            norm_stats(None, xin, first=True)
            norm_apply(None, hn, xin, first=True).then_inc(S["h_first"], 1)
            af = ring[:, 0:T, :]
            v.wait_ge(S["adj_in"], 16)
            link(v.tensor_copy(af, prior[:].bitcast(I32)))
            v.sem_inc(S["af_ready"], 1)
            link(v.tensor_reduce(rowmax[:], af, AX.X, ALU.max))
            v.tensor_reduce(amax[:, 0:1], rowmax[:], AX.X, ALU.max).then_inc(S["amax_t"], 1)
            v.tensor_scalar(maskN[:, 0:T // 2, :], af[:, 0:T // 2, :], 0.0, -BIG, ALU.is_equal, ALU.mult)
            v.tensor_scalar(empty3[:], rowmax[:], 0.0, None, ALU.is_le)
            v.wait_ge(S["weights_in"], n_weights)
            link(v.tensor_tensor(tA[:, 0:P], w1[:, 0:P], a1b[:, 0:P], ALU.mult))
            v.tensor_tensor(tA[:, P:2 * P], w1[:, 0:P], a1b[:, P:2 * P], ALU.mult)
            v.tensor_tensor(tB[:, 0:P], w3[:, 0:P], a3b[:, 0, :], ALU.mult)
            link(v.tensor_tensor(tB[:, P:2 * P], w3[:, 0:P], a3b[:, 1, :], ALU.mult))
            v.tensor_reduce(wa1[:], tA[:, 0:2 * P].rearrange("p (k o) -> p k o", k=2), AX.X, ALU.add)
            v.tensor_reduce(w3s[:], tB[:, 0:P].rearrange("p (h f) -> p h f", h=H3), AX.X, ALU.add)
            link(v.tensor_reduce(w3[:, P:P + H3], tB[:, P:2 * P].rearrange("p (h f) -> p h f", h=H3), AX.X, ALU.add))
            v.wait_ge(S["consts"], 1)
            v.tensor_copy(w3w[:, 0, :].rearrange("p (h f) -> p h f", h=H3), spread(w3[:, P:P + H3], DH3))
            v.tensor_copy(w3w[:, 1, :].rearrange("p (h f) -> p h f", h=H3), spread(w3s[:], DH3))
            v.tensor_copy(w1[:, P:P + 1], wa1[:, 1:2]).then_inc(S["wa_ready"], 1)
            link(v.tensor_scalar(beta3[:, 1:2], beta3[:, 0:1], -1.0, None, ALU.mult))
            v.tensor_scalar(beta3[:, 3:4], beta3[:, 0:1], 0.0, None, ALU.max)
            link(v.tensor_tensor(beta3[:, 1:2], beta3[:, 1:2], beta3[:, 0:1], ALU.max))
            v.sem_inc(S["beta_e"], 1)
            v.wait_ge(S["beta_ready"], 1)
            v.tensor_tensor(beta3[:, 2:3], beta3[:, 1:2], beta3[:, 3:4], ALU.add).then_inc(S["beta_e"], 1)
            v.wait_ge(S["amax_tr"], 1)
            v.tensor_reduce(amax[0:1, 1:2], acc[0:1, 0, 0:P], AX.X, ALU.max).then_inc(S["amax_row"], 1)
            v.wait_ge(S["amax_b"], 1)
            link(v.tensor_scalar(amax[:, 2:3], acc[:, 1, 0:1], 0.0, PRIOR_EPS, ALU.max, ALU.add))
            link(v.reciprocal(amax[:, 3:4], amax[:, 2:3]))
            link(v.tensor_scalar(amax[:, 4:5], amax[:, 3:4], PRIOR_EPS, None, ALU.mult))
            v.sem_inc(S["adjf"], 2)
            for c in range(T):
                v.wait_ge(S["adjT_psum"], c + 1)
                v.tensor_scalar(mask1[:, c, :], slot[c % 3], 0.0, None, ALU.is_gt)
                link(v.tensor_scalar(clipU[:, c, :], slot[c % 3], 0.0, E_HI, ALU.not_equal, ALU.mult))
                v.sem_inc(S["adjT_read"], 1)
                v.tensor_scalar(clipU[:, c, :], clipU[:, c, :], E_LO, None, ALU.max)
            link = Links(v, S["dve_link"])
            with v.Fori(0, B) as b:
                layer0(b)
                layer1(b)
                queries_keys2()
                layer2(b)
                layer3(b)
                end_graph(v, "go_v")


def kernel(**inputs):
    import concourse.bacc as bacc
    from concourse.bass_utils import run_bass_kernel_spmd

    nc = bacc.Bacc("TRN2", target_bir_lowering=False, num_devices=1)
    arrays, aps = {}, {}
    for name in INPUTS:
        arr = np.ascontiguousarray(inputs[name])
        if arr.ndim == 0:
            arr = arr.reshape(1, 1)
        arrays[f"in_{name}"] = arr
        aps[name] = nc.dram_tensor(f"in_{name}", arr.shape, mybir.dt.from_np(arr.dtype), kind="ExternalInput").ap()
    out = nc.dram_tensor("out_0", (B, N, D), F32, kind="ExternalOutput").ap()
    build(nc, aps, out)
    r = run_bass_kernel_spmd(nc, [arrays], core_ids=[0])
    return r.results[0]["out_0"]
```
